# Optimizing a Trainium2 kernel written in Bass

```python
import numpy as np
import jax
import jax.numpy as jnp

def _softmax(x, axis=-1):
    return jax.nn.softmax(x, axis=axis)

def _gelu(x):
    return jax.nn.gelu(x, approximate=True)

def _silu(x):
    return jax.nn.silu(x)

def _sigmoid(x):
    return jax.nn.sigmoid(x)

def _layernorm(x, axis=-1, eps=1e-05):
    m = jnp.mean(x, axis=axis, keepdims=True)
    v = jnp.var(x, axis=axis, keepdims=True)
    return (x - m) / jnp.sqrt(v + eps)

def _scatter_add(tgt, idx, src, axis=0):
    return tgt.at[idx].add(src)

def _segment_sum(src, seg, n):
    return jax.ops.segment_sum(src, seg, n)
kernel_name = 'mk_macaron_d1_jaxref_r8_5d2a1e'

def setup_inputs(seed: int=0):
    np.random.seed(seed)
    _w = jnp.asarray

    def _L0_attn_setup():
        import jax, jax.numpy as jnp
        import numpy as np
        import math
        N_HEAD = 16
        N_EMBD = 256
        HEAD_DIM = 128
        N_LAYER = 24
        EPS = 1e-05

        def _get_alibi_slopes(n_heads):

            def pow2(n):
                start = 2 ** (-2 ** (-(math.log2(n) - 3)))
                return [start * start ** i for i in range(n)]
            if math.log2(n_heads).is_integer():
                return pow2(n_heads)
            c = 2 ** math.floor(math.log2(n_heads))
            s = pow2(c)
            extra = _get_alibi_slopes(2 * c)
            return s + extra[0::2][:n_heads - c]
        ALIBI_SLOPES = jnp.asarray(np.array(_get_alibi_slopes(N_HEAD), dtype=np.float32))

        def rmsnorm(x, w, eps=EPS):
            xf = x.astype(jnp.float32)
            out = xf * jax.lax.rsqrt(jnp.mean(xf * xf, axis=-1, keepdims=True) + eps)
            return (out * w.astype(jnp.float32)).astype(x.dtype)
        key = jax.random.key(seed)
        ks = jax.random.split(key, 8)
        B, T, C, H, D = (2, 256, N_EMBD, N_HEAD, HEAD_DIM)
        sc = 1.0 / math.sqrt(C)
        proj_std = 0.5 / math.sqrt(C) / math.sqrt(N_LAYER)
        return {'x': jax.random.normal(ks[0], (B, T, C), jnp.float32), 'Wq': jax.random.normal(ks[1], (C, H * D), jnp.float32) * sc, 'Wk': jax.random.normal(ks[2], (C, H * D), jnp.float32) * sc, 'Wv': jax.random.normal(ks[3], (C, H * D), jnp.float32) * sc, 'Wproj': jax.random.normal(ks[4], (H * D, C), jnp.float32) * proj_std, 'q_rms_w': jnp.ones((D,), jnp.float32), 'k_rms_w': jnp.ones((D,), jnp.float32), 'subln_w': jnp.ones((D,), jnp.float32)}
    _L0_attn_in = _L0_attn_setup()

    def _L0_ffn_setup():
        import jax, jax.numpy as jnp
        import numpy as np
        B, S, DIM = (2, 256, 256)
        INTER = 176
        E = 8
        K = 2
        SHARED = 1
        ROUTE_SCALE = 1.0

        def _expert(xt, w1, w2, w3, cw=None):
            h = jax.nn.silu((xt @ w1.T).astype(jnp.float32)) * (xt @ w3.T).astype(jnp.float32)
            if cw is not None:
                h = cw[:, None] * h
            return h.astype(xt.dtype) @ w2.T
        key = jax.random.key(seed)
        ks = jax.random.split(key, 9)
        bf = lambda k, shape: (jax.random.normal(k, shape, dtype=jnp.float32) * 0.02).astype(jnp.bfloat16)
        return {'x': jax.random.normal(ks[0], (B, S, DIM), dtype=jnp.float32).astype(jnp.bfloat16), 'gate_w': jax.random.normal(ks[1], (E, DIM), dtype=jnp.float32) * 0.02, 'gate_b': jax.random.normal(ks[2], (E,), dtype=jnp.float32) * 0.01, 'w1': bf(ks[3], (E, INTER, DIM)), 'w2': bf(ks[4], (E, DIM, INTER)), 'w3': bf(ks[5], (E, INTER, DIM)), 'sw1': bf(ks[6], (SHARED * INTER, DIM)), 'sw2': bf(ks[7], (DIM, SHARED * INTER)), 'sw3': bf(ks[8], (SHARED * INTER, DIM))}
    _L0_ffn_in = _L0_ffn_setup()
    _d = {'L0_attn_x': _L0_attn_in['x'], 'L0_attn_Wq': _L0_attn_in['Wq'], 'L0_attn_Wk': _L0_attn_in['Wk'], 'L0_attn_Wv': _L0_attn_in['Wv'], 'L0_attn_Wproj': _L0_attn_in['Wproj'], 'L0_attn_q_rms_w': _L0_attn_in['q_rms_w'], 'L0_attn_k_rms_w': _L0_attn_in['k_rms_w'], 'L0_attn_subln_w': _L0_attn_in['subln_w'], 'L0_ffn_gate_w': _L0_ffn_in['gate_w'], 'L0_ffn_gate_b': _L0_ffn_in['gate_b'], 'L0_ffn_w1': _L0_ffn_in['w1'], 'L0_ffn_w2': _L0_ffn_in['w2'], 'L0_ffn_w3': _L0_ffn_in['w3'], 'L0_ffn_sw1': _L0_ffn_in['sw1'], 'L0_ffn_sw2': _L0_ffn_in['sw2'], 'L0_ffn_sw3': _L0_ffn_in['sw3']}
    _x0 = _d['L0_attn_x']
    _d['L0_attn_x'] = jax.random.normal(jax.random.fold_in(jax.random.key(seed), 1), (1, 1024, 256), dtype=_x0.dtype)
    del _x0
    return _d

def reference(L0_attn_x, L0_attn_Wq, L0_attn_Wk, L0_attn_Wv, L0_attn_Wproj, L0_attn_q_rms_w, L0_attn_k_rms_w, L0_attn_subln_w, L0_ffn_gate_w, L0_ffn_gate_b, L0_ffn_w1, L0_ffn_w2, L0_ffn_w3, L0_ffn_sw1, L0_ffn_sw2, L0_ffn_sw3):

    def _L0_attn_ref(x, Wq, Wk, Wv, Wproj, q_rms_w, k_rms_w, subln_w):
        import jax, jax.numpy as jnp
        import numpy as np
        import math
        N_HEAD = 16
        N_EMBD = 256
        HEAD_DIM = 128
        N_LAYER = 24
        EPS = 1e-05

        def _get_alibi_slopes(n_heads):

            def pow2(n):
                start = 2 ** (-2 ** (-(math.log2(n) - 3)))
                return [start * start ** i for i in range(n)]
            if math.log2(n_heads).is_integer():
                return pow2(n_heads)
            c = 2 ** math.floor(math.log2(n_heads))
            s = pow2(c)
            extra = _get_alibi_slopes(2 * c)
            return s + extra[0::2][:n_heads - c]
        ALIBI_SLOPES = jnp.asarray(np.array(_get_alibi_slopes(N_HEAD), dtype=np.float32))

        def rmsnorm(x, w, eps=EPS):
            xf = x.astype(jnp.float32)
            out = xf * jax.lax.rsqrt(jnp.mean(xf * xf, axis=-1, keepdims=True) + eps)
            return (out * w.astype(jnp.float32)).astype(x.dtype)
        B, T, C = x.shape
        H, D = (N_HEAD, HEAD_DIM)
        q = (x @ Wq).reshape(B, T, H, D)
        k = (x @ Wk).reshape(B, T, H, D)
        v = (x @ Wv).reshape(B, T, H, D)
        q = rmsnorm(q, q_rms_w)
        k = rmsnorm(k, k_rms_w)
        idx = jnp.arange(T)
        dist = jnp.maximum(idx[:, None] - idx[None, :], 0).astype(jnp.float32)
        bias = -dist[None, :, :] * ALIBI_SLOPES[:, None, None]
        causal = idx[:, None] >= idx[None, :]
        scale = 1.0 / math.sqrt(D)
        scores = jnp.einsum('bthd,bshd->bhts', q, k) * scale + bias[None]
        scores = jnp.where(causal[None, None], scores, -jnp.inf)
        attn = jax.nn.softmax(scores, axis=-1)
        y = jnp.einsum('bhts,bshd->bhtd', attn, v)
        y = rmsnorm(y, subln_w)
        y = y.transpose(0, 2, 1, 3).reshape(B, T, H * D)
        return y @ Wproj

    def _L0_ffn_ref(x, gate_w, gate_b, w1, w2, w3, sw1, sw2, sw3):
        import jax, jax.numpy as jnp
        import numpy as np
        B, S, DIM = (2, 256, 256)
        INTER = 176
        E = 8
        K = 2
        SHARED = 1
        ROUTE_SCALE = 1.0

        def _expert(xt, w1, w2, w3, cw=None):
            h = jax.nn.silu((xt @ w1.T).astype(jnp.float32)) * (xt @ w3.T).astype(jnp.float32)
            if cw is not None:
                h = cw[:, None] * h
            return h.astype(xt.dtype) @ w2.T
        Bx, Sx, D = x.shape
        xt = x.reshape(-1, D)
        T = xt.shape[0]
        scores = xt.astype(jnp.float32) @ gate_w.T
        scores = jnp.sqrt(jax.nn.softplus(scores))
        biased = scores + gate_b
        _, idx = jax.lax.top_k(biased, K)
        weights = jnp.take_along_axis(scores, idx, axis=1) * ROUTE_SCALE
        cw = jnp.einsum('tk,tke->te', weights, jax.nn.one_hot(idx, E, dtype=jnp.float32))
        y = jnp.zeros((T, D), dtype=xt.dtype)
        for e in range(E):
            y = y + _expert(xt, w1[e], w2[e], w3[e], cw[:, e])
        z = _expert(xt, sw1, sw2, sw3)
        return (y + z).reshape(Bx, Sx, D)
    x = L0_attn_x
    x = x + 0.5 * _L0_ffn_ref(_layernorm(x, axis=-1), L0_ffn_gate_w, L0_ffn_gate_b, L0_ffn_w1, L0_ffn_w2, L0_ffn_w3, L0_ffn_sw1, L0_ffn_sw2, L0_ffn_sw3)
    x = x + _L0_attn_ref(_layernorm(x, axis=-1), L0_attn_Wq, L0_attn_Wk, L0_attn_Wv, L0_attn_Wproj, L0_attn_q_rms_w, L0_attn_k_rms_w, L0_attn_subln_w)
    x = x + 0.5 * _L0_ffn_ref(_layernorm(x, axis=-1), L0_ffn_gate_w, L0_ffn_gate_b, L0_ffn_w1, L0_ffn_w2, L0_ffn_w3, L0_ffn_sw1, L0_ffn_sw2, L0_ffn_sw3)
    return x

_drawn_inputs = setup_inputs


def setup_inputs(seed=0):
    import zlib

    import numpy as np

    out = dict(_drawn_inputs(seed))
    spreads = {'L0_attn_q_rms_w': (1.0, 0.2),
     'L0_attn_k_rms_w': (1.0, 0.2),
     'L0_attn_subln_w': (1.0, 0.2)}
    factors = {'L0_ffn_gate_w': 3.739,
     'L0_ffn_gate_b': 8.0,
     'L0_ffn_w1': 3.248,
     'L0_ffn_w2': 3.208,
     'L0_ffn_w3': 3.212,
     'L0_ffn_sw1': 4.285,
     'L0_ffn_sw2': 4.226,
     'L0_ffn_sw3': 4.21}
    for name, (base, spread) in spreads.items():
        noise = np.random.default_rng([zlib.crc32(name.encode()), seed]).standard_normal(out[name].shape)
        drawn = base * np.exp(spread * noise) if base else spread * noise
        out[name] = jnp.asarray(drawn.astype(out[name].dtype))
    for name, factor in factors.items():
        out[name] = (out[name] * factor).astype(out[name].dtype)
    return out
```

```python
from contextlib import ExitStack

import numpy as np

import concourse.bass as bass
from concourse import mybir

F32 = mybir.dt.float32
F32R = mybir.dt.float32r
BF16 = mybir.dt.bfloat16
ALU = mybir.AluOpType
ACT = mybir.ActivationFunctionType
AX_X = mybir.AxisListType.X

P = 128
EPS = 1e-5
MASKED = 1e30
LN_FLOOR = 60
BANK = 512


def need(engine, semaphore, count):
    if not isinstance(count, int) or count > 0:
        engine.wait_ge(semaphore, count)


def macaron_kernel(nc, x_in, w_qkv, w_proj, q_w, k_w, y_w, gate_w, gate_b, w_up_a, w_up_b, w_down, out):
    T, C = x_in.shape
    H = w_qkv.shape[0]
    D = P
    E = gate_w.shape[1]
    J = w_down.shape[0]
    INTER = J // (E + 1)
    TB = T // P
    CC = C // P
    JT = -(-J // P)
    JPAD = JT * P
    JTAIL = J - (JT - 1) * P
    HB = TB // 2
    HT = T // 2
    assert (T, C, D) == (1024, 256, 128) and HT == BANK

    SLOPE = [2.0 ** (-8.0 / H * (h + 1)) for h in range(2)]
    SLOPE_STEP = 2.0 ** (-8.0 / H * 2)
    QSCALE = -float(D) ** -0.5

    CHUNKS = [[(c, min(4, t + 1 - c)) for c in range(0, t + 1, 4)] for t in range(TB)]
    FIRST = [sum(len(CHUNKS[u]) for u in range(t)) for t in range(TB)]
    NCH = sum(len(c) for c in CHUNKS)

    with ExitStack() as ctx:
        def sb(name, shape, dt=F32):
            return ctx.enter_context(nc.sbuf_tensor(name, shape, dt))

        def sem(name):
            return ctx.enter_context(nc.semaphore(name))

        x = sb("x", [P, TB, C])
        xT_hi = sb("xT_hi", [P, CC, T], F32R)
        xT_lo = sb("xT_lo", [P, CC, T], F32R)
        ident = sb("ident", [P, P])
        ROW_AT = [18, 12, 15, 8, 0, 15, 8, 0]
        srow = sb("srow", [P, 21 * P])
        xn = srow[:, 0:TB * C].rearrange("p (b c) -> p b c", c=C)
        stage_a = srow[:, 0:TB * C].bitcast(BF16)[:, 0:CC * J].rearrange("p (c j) -> p c j", c=CC)
        pT_hi = sb("pT_hi", [P, 2, T], F32R)
        pT_lo = sb("pT_lo", [P, 2, T], F32R)
        qkv = sb("qkv", [P, TB, 3 * D])
        sq = sb("sq", [P, HB, 2 * D])
        qT_hi = sb("qT_hi", [P, 2, T], F32R)
        qT_lo = sb("qT_lo", [P, 2, T], F32R)
        kT_hi = sb("kT_hi", [P, 2, T], F32R)
        kT_lo = sb("kT_lo", [P, 2, T], F32R)
        v_hi = sb("v_hi", [P, 2, TB, D], F32R)
        v_lo = sb("v_lo", [P, 2, TB, D], F32R)
        raw = sb("raw", [P, 2 * (CC * 3 * D + C)])
        wraw = raw[:, 0:2 * CC * 3 * D].rearrange("p (a c d) -> p a c d", a=2, c=CC)
        wpraw = raw[:, 2 * CC * 3 * D:].rearrange("p (a c) -> p a c", a=2)
        stage_d = raw[:, :].bitcast(BF16)[:, 0:JT * C].rearrange("p (t c) -> p t c", t=JT)
        w_hi = sb("w_hi", [P, CC, 3 * D], F32R)
        w_lo = sb("w_lo", [P, CC, 3 * D], F32R)
        wp_hi = sb("wp_hi", [P, C], F32R)
        wp_lo = sb("wp_lo", [P, C], F32R)
        alibi = sb("alibi", [P, 2, T])
        stage_b = alibi[:, :, :].rearrange("p a t -> p (a t)").bitcast(BF16)[:, 0:CC * J].rearrange(
            "p (c j) -> p c j", c=CC)
        yrow = sb("yrow", [P, 2, HB, D])
        ysq = sb("ysq", [P, HB, D])
        yT_hi = sb("yT_hi", [P, 2, BANK], F32R)
        yT_lo = sb("yT_lo", [P, 2, BANK], F32R)
        up_a = sb("up_a", [P, CC, JPAD], F32R)
        up_b = sb("up_b", [P, CC, JPAD], F32R)
        down = sb("down", [P, JT, C], F32R)
        expert_of = sb("expert_of", [P, JPAD], F32R)
        cwT = qT_hi[:, 0, :]
        gt = ysq[:, :, :].rearrange("p b (e f) -> p (b e) f", f=E)
        eq = yrow[:, 0, :, :].rearrange("p b (e f) -> p (b e) f", f=E)
        flat = qkv[:, :, :].rearrange("p b d -> p (b d)")
        ff_s = flat[:, 0:2 * BANK].rearrange("p (r t) -> p r t", r=2)
        ff_m = flat[:, 2 * BANK:4 * BANK].rearrange("p (r t) -> p r t", r=2)
        ff_h = flat[:, 4 * BANK:6 * BANK].rearrange("p (r t) -> p r t", r=2)
        hT_hi = pT_hi[:, :, :].rearrange("p a (r t) -> p (a r) t", t=BANK)
        hT_lo = pT_lo[:, :, :].rearrange("p a (r t) -> p (a r) t", t=BANK)
        HRING = 3
        cw_rows = sq[:, :, :].rearrange("p a (r e) -> p (a r) e", e=P)
        expert_f = yrow[:, :, :, :].rearrange("p a b d -> p (a b d)")

        bn = sb("bn", [P, TB, 6])
        mv = sb("mv", [P, TB, 2])
        lnv = sb("lnv", [P, TB])
        rstd = sb("rstd", [P, TB])
        qk_ss = sb("qk_ss", [P, 2, HB * 2])
        qk_ln = sb("qk_ln", [P, 2, HB * 2])
        qk_r = sb("qk_r", [P, 2, HB * 2])
        y_ss = sb("y_ss", [P, 2, HB])
        y_e = sb("y_e", [P, 2, HB])
        y_t = sb("y_t", [P, 2, HB])
        y_ln = sb("y_ln", [P, 2, HB])
        y_f = sb("y_f", [P, 2, HB])
        neg_max = sb("neg_max", [P, 2, TB])
        row_sum = sb("row_sum", [P, 2, TB])
        q_w_sb = sb("q_w_sb", [P, 1])
        q_scale = sb("q_scale", [P, 1])
        k_scale = sb("k_scale", [P, 1])
        y_scale = sb("y_scale", [P, 1])
        epst = sb("epst", [P, 1])
        slope_step = sb("slope_step", [P, 1])
        carrier = sb("carrier", [P, 1])
        gw = sb("gw", [P, CC, E])
        gw2 = sb("gw2", [P, CC, 2 * E], F32R)
        gb = sb("gb", [P, TB * E])
        lower = sb("lower", [P, E, E])
        R = {n: sb("r_" + n, [P, TB * E]) for n in
             ("z", "a", "u", "w", "lw", "d", "i", "rd", "v", "sp", "L", "mn", "s", "b")}
        R |= {"rank": R["d"], "cw": R["w"]}

        ps = ctx.enter_context(nc.psum_tensor("ps", [P, 8, BANK], F32))
        PT_BANK, M_BANK, X_BANK, Y_BANK = 2, 4, 6, 7
        A_BANK, B_BANK, G_BANK, ACC_BANK = 0, 2, 4, 6
        scores = ps[:, 0:2, :].rearrange("p a t -> p (a t)")

        s_x = [sem(f"s_x{i}") for i in range(2)]
        s_small = sem("s_small")
        s_in_a, s_in_b, s_in_d = sem("s_in_a"), sem("s_in_b"), sem("s_in_d")
        s_w = [sem(f"s_w{i}") for i in range(2)]
        s_wp = [sem(f"s_wp{i}") for i in range(2)]
        s_expert = sem("s_expert")
        s_out = sem("s_out")
        s_zeroed, s_const = sem("s_zeroed"), sem("s_const")
        s_cwzero, s_cwone = sem("s_cwzero"), sem("s_cwone")
        s_escratch, s_eof, s_dist, s_cast_d = sem("s_escratch"), sem("s_eof"), sem("s_dist"), sem("s_cast_d")
        s_alibi = sem("s_alibi")
        s_sq, s_qkn = sem("s_sq"), sem("s_qkn")
        s_ysq, s_yn = sem("s_ysq"), sem("s_yn")
        s_wlo, s_wplo = sem("s_wlo"), sem("s_wplo")
        s_cast_a = sem("s_cast_a")
        s_lnv, s_rstd, s_xThi = sem("s_lnv"), sem("s_rstd"), sem("s_xThi")
        s_rt_act, s_cwhi = sem("s_rt_act"), sem("s_cwhi")
        s_silu, s_hhi = sem("s_silu"), sem("s_hhi")
        s_exp, s_pthi, s_row = sem("s_exp"), sem("s_pthi"), sem("s_row")
        s_qkln, s_qkr, s_xhi, s_vhi = sem("s_qkln"), sem("s_qkr"), sem("s_xhi"), sem("s_vhi")
        s_yrow, s_yln, s_yf = sem("s_yrow"), sem("s_yln"), sem("s_yf")
        s_whi, s_wphi = sem("s_whi"), sem("s_wphi")
        s_cast_b, s_gw, s_qs = sem("s_cast_b"), sem("s_gw"), sem("s_qs")
        s_bn, s_mv, s_xn, s_xTlo = sem("s_bn"), sem("s_mv"), sem("s_xn"), sem("s_xTlo")
        s_rt_dve, s_cwT = sem("s_rt_dve"), sem("s_cwT")
        s_m, s_h, s_hlo, s_acc = sem("s_m"), sem("s_h"), sem("s_hlo"), sem("s_acc")
        s_ttr, s_ptlo, s_qkss, s_xlo = sem("s_ttr"), sem("s_ptlo"), sem("s_qkss"), sem("s_xlo")
        s_yss, s_ye, s_yt, s_vlo, s_pjadd = sem("s_yss"), sem("s_ye"), sem("s_yt"), sem("s_vlo"), sem("s_pjadd")
        s_xtr, s_logit, s_cwtr = sem("s_xtr"), sem("s_logit"), sem("s_cwtr")
        s_a, s_b, s_g, s_down = sem("s_a"), sem("s_b"), sem("s_g"), sem("s_down")
        s_scored, s_pt, s_pv, s_qkv = sem("s_scored"), sem("s_pt"), sem("s_pv"), sem("s_qkv")
        s_xt, s_pj = sem("s_xt"), sem("s_pj")

        RT_DVE, RT_ACT = 22, 5

        block = ctx.enter_context(nc.Block())

        KB, QB, YB, KA, QA, YA = range(6)

        def xuse(i, pos):
            if isinstance(i, int) and i < 1:
                return {-1: {KA: 0, QA: 1}, 0: {KB: 2, QB: 3, KA: 4, QA: 5, YA: 6}}[i][pos]
            if isinstance(i, int) and i >= H - 1:
                n = 1 + 6 * (H - 1)
                return {H - 1: {KB: n, QB: n + 1, YB: n + 2, YA: n + 3}, H: {YB: n + 4}}[i][pos]
            return 1 + 6 * i + pos

        def run_heads(engine, body):
            for i in (-1, 0, 1):
                body(i, i // 2, i % 2)
            with engine.Fori(1, H // 2 - 1) as it:
                body(2 * it, it, 0)
                body(2 * it + 1, it, 1)
            for i in (H - 2, H - 1, H):
                body(i, i // 2, i % 2)

        def parts(i):
            if not isinstance(i, int):
                return True, True, True, True
            return 0 <= i < H, i + 1 < H, i >= 1, i + 2 < H

        @block.sync
        def _(sp):
            sp.dma_start(x[:, 0:HB, :], x_in[0:HT, :].rearrange("(b p) c -> p b c", p=P)).then_inc(s_x[0], 16)
            sp.dma_start(x[:, HB:, :], x_in[HT:, :].rearrange("(b p) c -> p b c", p=P)).then_inc(s_x[1], 16)
            for dst, src in ((gw[:, :, :], gate_w.rearrange("(c p) e -> p c e", p=P)), (gb[:, :], gate_b),
                             (q_w_sb[:, :], q_w), (k_scale[:, :], k_w), (y_scale[:, :], y_w)):
                sp.dma_start(dst, src).then_inc(s_small, 16)
            sp.dma_start(stage_b, w_up_b.rearrange("(c p) j -> p c j", p=P)).then_inc(s_in_b, 16)
            sp.dma_start(stage_d[:, 0:JT - 1, :],
                         w_down[0:(JT - 1) * P, :].rearrange("(t p) c -> p t c", p=P)).then_inc(s_in_d, 16)
            sp.wait_ge(s_zeroed, 3)
            sp.dma_start(stage_d[0:JTAIL, JT - 1, :], w_down[(JT - 1) * P:, :]).then_inc(s_in_d, 16)
            sp.wait_ge(s_xtr, 4)
            sp.dma_start(stage_a, w_up_a.rearrange("(c p) j -> p c j", p=P)).then_inc(s_in_a, 16)

            sp.wait_ge(s_eof, 2)
            sp.dma_start(expert_of[32:32 + E + 1, :].bitcast(F32), expert_of[0:E + 1, :].bitcast(F32)).then_inc(s_expert, 16)

            def load_w(n, slot):
                need(sp, s_wlo, n - 1)
                sp.dma_start(wraw[:, slot, :, :], w_qkv[n, :, :, :]).then_inc(s_w[slot], 16)

            def load_wp(n, slot):
                need(sp, s_wplo, n - 1)
                sp.dma_start(wpraw[:, slot, :], w_proj[n, :, :]).then_inc(s_wp[slot], 16)

            sp.wait_ge(s_cast_d, 1)
            for n in range(2):
                load_w(n, n)
                load_wp(n, n)
            for n in (2, 3):
                load_w(n, n % 2)
            with sp.Fori(2, H // 2) as it:
                for slot in range(2):
                    load_w(2 * it + slot, slot)
                    load_wp(2 * it + slot - 2, slot)
            for n in (H - 2, H - 1):
                load_wp(n, n % 2)
            for half in range(2):
                sp.wait_ge(s_acc, 2 * 3 + 2 * half)
                sp.dma_start(out[half * HT:(half + 1) * HT, :].rearrange("(b p) c -> p b c", p=P),
                             x[:, half * HB:(half + 1) * HB, :]).then_inc(s_out, 16)
            sp.wait_ge(s_out, 32)

        @block.gpsimd
        def _(pool):
            pool.memset(ident[:, :], 0.0).then_inc(s_zeroed, 1)
            pool.wait_ge(s_zeroed, 1)
            pool.affine_select(out=ident[:, :], in_=ident[:, :], compare_op=ALU.not_equal, fill=1.0, base=0,
                               pattern=[[-1, P]], channel_multiplier=1).then_inc(s_const, 1)
            pool.memset(epst[:, :], EPS).then_inc(s_const, 1)
            pool.memset(slope_step[:, :], SLOPE_STEP)
            pool.memset(lower[:, :, :], 1.0).then_inc(s_zeroed, 1)
            pool.wait_ge(s_zeroed, 2)
            pool.affine_select(out=lower[:, :, :], in_=lower[:, :, :], compare_op=ALU.is_gt, fill=0.0, base=0,
                               pattern=[[1, E], [-1, E]], channel_multiplier=0).then_inc(s_const, 1)
            pool.memset(up_a[:, :, J:JPAD].bitcast(F32), 0.0)
            pool.memset(up_b[:, :, J:JPAD].bitcast(F32), 0.0)
            pool.memset(stage_d[:, JT - 1, :], 0.0).then_inc(s_zeroed, 1)

            def clear_combine_rows(f):
                need(pool, s_qkss, 2 * H * f)
                pool.memset(cw_rows[:, :, :], 0.0).then_inc(s_cwzero, 1)
                pool.wait_ge(s_cwzero, f + 1)
                for r in (0, 32):
                    last = pool.memset(cw_rows[:, :, r + E:r + E + 1], 1.0)
                last.then_inc(s_cwone, 1)

            clear_combine_rows(0)
            for n, lo in enumerate(range(0, JPAD, T)):
                k = min(T, JPAD - lo)
                need(pool, s_eof, n)
                pool.memset(expert_f[:, 0:k], 1.0).then_inc(s_escratch, 1)
                pool.wait_ge(s_escratch, 2 * n + 1)
                pool.affine_select(out=expert_f[:, 0:k], in_=expert_f[:, 0:k], compare_op=ALU.is_ge, fill=0.0,
                                   base=lo, pattern=[[1, k]], channel_multiplier=-INTER).then_inc(s_escratch, 1)
                pool.wait_ge(s_escratch, 2 * n + 2)
                pool.affine_select(out=expert_of[:, lo:lo + k], in_=expert_f[:, 0:k], compare_op=ALU.is_ge, fill=0.0,
                                   base=INTER - 1 - lo, pattern=[[-1, k]], channel_multiplier=INTER).then_inc(s_eof, 1)
            pool.wait_ge(s_in_d, 32)
            pool.tensor_copy(down[:, :, :], stage_d[:, :, :]).then_inc(s_cast_d, 1)
            pool.wait_ge(s_cast_b, 1)
            dist = alibi[:, 1, :]
            pool.iota(dist, pattern=[[-1, T]], base=T - P, channel_multiplier=1,
                      allow_small_or_imprecise_dtypes=True).then_inc(s_dist, 1)
            pool.wait_ge(s_dist, 1)
            pool.affine_select(out=dist, in_=dist, compare_op=ALU.is_ge, fill=MASKED, base=T - P,
                               pattern=[[-1, T]], channel_multiplier=1).then_inc(s_dist, 1)
            pool.wait_ge(s_dist, 2)
            pool.tensor_scalar(alibi[:, 0, :], dist, SLOPE[0], None, ALU.mult).then_inc(s_alibi, 1)
            pool.tensor_scalar(dist, dist, SLOPE[1], None, ALU.mult).then_inc(s_alibi, 1)

            def split_w(n, slot):
                pool.wait_ge(s_whi, n + 1)
                pool.tensor_tensor(w_lo[:, :, :], wraw[:, slot, :, :], w_hi[:, :, :].bitcast(F32), ALU.subtract)\
                    .then_inc(s_wlo, 1)

            def square_qk(n, half):
                pool.wait_ge(s_row, TB * n + HB * (half + 1))
                need(pool, s_qkss, 2 * n + half)
                qk = qkv[:, half * HB:(half + 1) * HB, 0:2 * D]
                pool.tensor_tensor(sq[:, :, :], qk, qk, ALU.mult).then_inc(s_sq, 1)

            def scale_qk(n, half):
                pool.wait_ge(s_qkr, 2 * n + half + 1)
                qk = qkv[:, half * HB:(half + 1) * HB, 0:2 * D].rearrange("p b (a d) -> p b a d", a=2)
                r = qk_r[:, half, :].rearrange("p (b a) -> p b a", a=2).unsqueeze(3).to_broadcast([P, HB, 2, D])
                pool.tensor_tensor(qk, qk, r, ALU.mult).then_inc(s_qkn, 1)

            def square_y(h, half):
                pool.wait_ge(s_yrow, 2 * h + half + 1)
                need(pool, s_yss, 2 * h + half)
                pool.tensor_tensor(ysq[:, :, :], yrow[:, half, :, :], yrow[:, half, :, :], ALU.mult)\
                    .then_inc(s_ysq, 1)

            def scale_y(h, half):
                pool.wait_ge(s_yf, 2 * h + half + 1)
                f = y_f[:, half, :].unsqueeze(2).to_broadcast([P, HB, D])
                pool.tensor_tensor(yrow[:, half, :, :], yrow[:, half, :, :], f, ALU.mult).then_inc(s_yn, 1)

            split_w(0, 0)
            step_t = slope_step[:, :]

            def body(i, it, par):
                att, nxt, prev, after = parts(i)
                n = i + 1
                if prev and nxt:
                    pool.wait_ge(s_ttr, TB * i)
                    pool.tensor_tensor(alibi[:, 1 - par, :], alibi[:, 1 - par, :], step_t.to_broadcast([P, T]), ALU.mult)\
                        .then_inc(s_alibi, 1)
                if prev:
                    square_y(i - 1, 1)
                if nxt:
                    square_qk(n, 0)
                if prev:
                    pool.wait_ge(s_wphi, i)
                    pool.tensor_tensor(wp_lo[:, :], wpraw[:, 1 - par, :], wp_hi[:, :].bitcast(F32), ALU.subtract)\
                        .then_inc(s_wplo, 1)
                    scale_y(i - 1, 1)
                if nxt:
                    scale_qk(n, 0)
                    square_qk(n, 1)
                if att:
                    square_y(i, 0)
                if nxt:
                    scale_qk(n, 1)
                if after:
                    split_w(i + 2, par)
                if att:
                    scale_y(i, 0)

            run_heads(pool, body)
            clear_combine_rows(1)

        @block.scalar
        def _(act):
            def layer_norm(k):
                act.wait_ge(s_mv, k + 1)
                act.activation(lnv[:, :], mv[:, :, 1], ACT.Ln, bias=epst[:, :]).then_inc(s_lnv, 1)
                act.wait_ge(s_lnv, k + 1)
                act.activation(rstd[:, :], lnv[:, :], ACT.Exp, scale=-0.5).then_inc(s_rstd, 1)
                for half in range(2):
                    for c in range(CC):
                        act.wait_ge(s_xtr, 4 * k + 2 * half + c + 1)
                        act.activation(xT_hi[:, c, half * HT:(half + 1) * HT], ps[:, 2 * half + c, :], ACT.Copy)\
                            .then_inc(s_xThi, 1)

            def ffn(f):
                base = RT_DVE * f
                for n, (name, src, func, scale, after_dve) in enumerate((
                        ("a", "z", ACT.Abs, 1.0, 2), ("u", "a", ACT.Exp, -1.0, 2), ("lw", "w", ACT.Ln, 1.0, 3),
                        ("L", "sp", ACT.Ln, 1.0, 12), ("s", "L", ACT.Exp, 0.5, 14))):
                    act.wait_ge(s_rt_dve, base + after_dve)
                    if n == 1:
                        act.wait_ge(s_rt_act, RT_ACT * f + 1)
                    act.activation(R[name][:, :], R[src][:, :], func, scale=scale).then_inc(s_rt_act, 1)
                act.preload_act_table_set("silu_and_others")
                act.wait_ge(s_cwtr, f + 1)
                act.activation(cwT[:, :], ps[:, G_BANK:G_BANK + 2, :].rearrange("p a t -> p (a t)"), ACT.Copy)\
                    .then_inc(s_cwhi, 1)

                def hi(g):
                    act.wait_ge(s_h, g + 1)
                    need(act, s_down, g - HRING + 1)
                    act.activation(hT_hi[:, g % HRING, :], ff_h[:, g % 2, :], ACT.Copy).then_inc(s_hhi, 1)

                for u in range(2 * JT):
                    g = 2 * JT * f + u
                    act.wait_ge(s_a, g + 1)
                    need(act, s_m, g - 1)
                    act.activation(ff_s[:, g % 2, :], ps[:, A_BANK + g % 2, :], ACT.Silu).then_inc(s_silu, 1)
                    if u:
                        hi(g - 1)
                hi(2 * JT * (f + 1) - 1)

            act.preload_act_table_set("natural_log_exp_and_others")
            layer_norm(0)
            act.wait_ge(s_in_a, 16)
            act.activation(up_a[:, :, 0:J], stage_a, ACT.Copy).then_inc(s_cast_a, 1)
            ffn(0)
            act.preload_act_table_set("natural_log_exp_and_others")
            layer_norm(1)

            def split_w(n, slot, use):
                act.wait_ge(s_w[slot], 16 * (use + 1))
                need(act, s_qkv, TB * n)
                act.activation(w_hi[:, :, :], wraw[:, slot, :, :], ACT.Copy).then_inc(s_whi, 1)

            def exp(i, par, t):
                act.wait_ge(s_ttr, TB * i + t + 1)
                row = srow[:, P * ROW_AT[t]:P * (ROW_AT[t] + t + 1)]
                act.activation(row, row, ACT.Exp, bias=neg_max[:, par, t:t + 1], scale=-1.0,
                               accum_out=row_sum[:, par, t:t + 1]).then_inc(s_exp, 1)

            def qkv_row(n, tb):
                act.wait_ge(s_qkv, TB * n + tb + 1)
                if tb == 0:
                    need(act, s_vlo, n)
                act.activation(qkv[:, tb, :], ps[:, M_BANK + tb % 2, 0:3 * D], ACT.Copy).then_inc(s_row, 1)

            def pt_hi(i, t):
                for c, (b0, nb) in enumerate(CHUNKS[t]):
                    ch = NCH * i + FIRST[t] + c
                    act.wait_ge(s_pt, ch + 1)
                    act.activation(pT_hi[:, t % 2, b0 * P:(b0 + nb) * P],
                                   ps[:, PT_BANK + (FIRST[t] + c) % 2, 0:nb * P], ACT.Copy).then_inc(s_pthi, 1)

            def x_hi(use, dst, scale):
                act.wait_ge(s_xt, use + 1)
                act.activation(dst, ps[:, X_BANK, :], ACT.Copy, scale=scale[:, :]).then_inc(s_xhi, 1)

            def half_of(tile, par, half):
                return tile[:, par, half * HT:(half + 1) * HT]

            def qk_rsqrt(n, half):
                act.wait_ge(s_qkss, 2 * n + half + 1)
                act.activation(qk_ln[:, half, :], qk_ss[:, half, :], ACT.Ln, scale=1.0 / D, bias=epst[:, :])\
                    .then_inc(s_qkln, 1)
                act.wait_ge(s_qkln, 2 * n + half + 1)
                act.activation(qk_r[:, half, :], qk_ln[:, half, :], ACT.Exp, scale=-0.5).then_inc(s_qkr, 1)

            def y_row(h, half):
                act.wait_ge(s_pv, TB * h + HB * (half + 1))
                act.activation(yrow[:, half, :, :].rearrange("p b d -> p (b d)"), ps[:, Y_BANK, :], ACT.Copy)\
                    .then_inc(s_yrow, 1)

            def y_rsqrt(h, half):
                act.wait_ge(s_yt, 2 * h + half + 1)
                act.activation(y_ln[:, half, :], y_t[:, half, :], ACT.Ln).then_inc(s_yln, 1)
                act.wait_ge(s_yln, 2 * h + half + 1)
                act.activation(y_f[:, half, :], y_ln[:, half, :], ACT.Exp, scale=-0.5).then_inc(s_yf, 1)

            split_w(0, 0, 0)
            act.wait_ge(s_qs, 1)

            def body(i, it, par):
                att, nxt, prev, after = parts(i)
                n = i + 1
                for t in range(TB):
                    if att:
                        pt_hi(i, t)
                    if prev and t == 0:
                        y_row(i - 1, 1)
                    if att and t == 5:
                        y_row(i, 0)
                    if att and t < 2:
                        dst, pos, scale = ((kT_hi, KB, k_scale), (qT_hi, QB, q_scale))[t]
                        x_hi(xuse(i, pos), half_of(dst, par, 1), scale)
                    if nxt and t < HB:
                        qkv_row(n, 2 * t)
                        qkv_row(n, 2 * t + 1)
                    if att and t < TB - 2:
                        exp(i, par, t + 2)
                    if nxt and t >= TB - 2:
                        exp(n, 1 - par, t - (TB - 2))
                    if prev and t == 1:
                        wp_use = it - 1 + (par + 1) // 2
                        act.wait_ge(s_wp[1 - par], 16 * (wp_use + 1))
                        need(act, s_pj, 4 * (i - 1))
                        act.activation(wp_hi[:, :], wpraw[:, 1 - par, :], ACT.Copy).then_inc(s_wphi, 1)
                    if prev and t == 2:
                        y_rsqrt(i - 1, 1)
                    if nxt and t == 3:
                        qk_rsqrt(n, 0)
                    if prev and t == 3:
                        x_hi(xuse(i, YB), yT_hi[:, 1, :], y_scale)
                    if nxt and t == 4:
                        act.activation(v_hi[:, 1 - par, :, :], qkv[:, :, 2 * D:3 * D], ACT.Copy).then_inc(s_vhi, 1)
                        x_hi(xuse(i, KA), half_of(kT_hi, 1 - par, 0), k_scale)
                    if nxt and t == 5:
                        qk_rsqrt(n, 1)
                        x_hi(xuse(i, QA), half_of(qT_hi, 1 - par, 0), q_scale)
                    if after and t == 5:
                        split_w(i + 2, par, it + 1)
                    if att and t == 6:
                        y_rsqrt(i, 0)
                    if att and t == 7:
                        x_hi(xuse(i, YA), yT_hi[:, 0, :], y_scale)

            run_heads(act, body)
            layer_norm(2)
            ffn(1)

        @block.vector
        def _(dve):
            dve.wait_ge(s_const, 3)
            dve.wait_ge(s_small, 80)
            dve.tensor_copy(gw2[:, :, 0:E], gw[:, :, :]).then_inc(s_gw, 1)
            dve.tensor_scalar(q_scale[:, :], q_w_sb[:, :], QSCALE, None, ALU.mult).then_inc(s_qs, 1)
            dve.wait_ge(s_gw, 1)
            dve.tensor_tensor(gw2[:, :, E:2 * E], gw[:, :, :], gw2[:, :, 0:E].bitcast(F32), ALU.subtract)\
                .then_inc(s_gw, 1)

            def layer_norm(k):
                for tb in range(TB):
                    if k == 0 and tb % HB == 0:
                        dve.wait_ge(s_x[tb // HB], 16)
                    last = dve.bn_stats(bn[:, tb, :], x[:, tb, :])
                last.then_inc(s_bn, 1)
                dve.wait_ge(s_bn, k + 1)
                for tb in range(TB):
                    last = dve.bn_aggr(mv[:, tb, :], bn[:, tb, :])
                last.then_inc(s_mv, 1)
                dve.wait_ge(s_rstd, k + 1)
                for tb in range(TB):
                    dve.tensor_scalar(xn[:, tb, :], x[:, tb, :], mv[:, tb, 0:1], rstd[:, tb:tb + 1],
                                      ALU.subtract, ALU.mult).then_inc(s_xn, 1)
                for half in range(2):
                    for c in range(CC):
                        dve.wait_ge(s_xThi, 4 * k + 2 * half + c + 1)
                        dst = (slice(None), c, slice(half * HT, (half + 1) * HT))
                        dve.tensor_tensor(xT_lo[dst], ps[:, 2 * half + c, :], xT_hi[dst].bitcast(F32), ALU.subtract)\
                            .then_inc(s_xTlo, 1)

            def ffn(f):
                steps = [RT_DVE * f]

                def step(instruction, wait=True):
                    instruction.then_inc(s_rt_dve, 1)
                    steps[0] += 1
                    if wait:
                        dve.wait_ge(s_rt_dve, steps[0])

                def after_act(n):
                    dve.wait_ge(s_rt_act, RT_ACT * f + n)

                r = {name: tile[:, :] for name, tile in R.items()}
                logits = ps[:, G_BANK, 0:TB * 2 * E].rearrange("p (b e) -> p b e", b=TB)
                by_block = R["v"][:, :].rearrange("p (b e) -> p b e", b=TB)
                dve.wait_ge(s_logit, f + 1)
                step(dve.tensor_copy(by_block, logits[:, :, E:2 * E]))
                step(dve.tensor_tensor(R["z"][:, :].rearrange("p (b e) -> p b e", b=TB), logits[:, :, 0:E],
                                       by_block, ALU.add))
                after_act(2)
                step(dve.tensor_scalar(r["w"], r["u"], 1.0, None, ALU.add))
                step(dve.tensor_scalar(r["d"], r["w"], -1.0, None, ALU.add))
                step(dve.tensor_scalar(r["i"], r["d"], 0.0, None, ALU.is_equal))
                step(dve.tensor_tensor(r["d"], r["d"], r["i"], ALU.add))
                step(dve.reciprocal(r["rd"], r["d"]))
                after_act(3)
                step(dve.tensor_tensor(r["lw"], r["lw"], r["i"], ALU.add))
                step(dve.tensor_tensor(r["v"], r["u"], r["lw"], ALU.mult))
                step(dve.tensor_tensor(r["v"], r["v"], r["rd"], ALU.mult))
                step(dve.scalar_tensor_tensor(r["sp"], r["z"], 0.0, r["v"], ALU.max, ALU.add))
                step(dve.tensor_scalar(r["sp"], r["sp"], 2.0 ** -LN_FLOOR, None, ALU.max))
                step(dve.tensor_scalar(r["mn"], r["z"], LN_FLOOR * float(np.log(2.0)), 0.0, ALU.add, ALU.min))
                after_act(4)
                step(dve.tensor_tensor(r["L"], r["L"], r["mn"], ALU.add))
                after_act(5)
                step(dve.tensor_tensor(r["b"], r["s"], gb[:, :], ALU.add))
                b = R["b"][:, :].rearrange("p (b e) -> p b e", b=TB)
                other = b.unsqueeze(2).to_broadcast([P, TB, E, E])
                own = b.unsqueeze(3).to_broadcast([P, TB, E, E])
                gt4, eq4 = (t[:, :, :].rearrange("p (b e) f -> p b e f", b=TB) for t in (gt, eq))
                dve.wait_ge(s_eof, 2)
                step(dve.tensor_tensor(gt4, other, own, ALU.is_gt), wait=False)
                step(dve.tensor_tensor(eq4, other, own, ALU.is_equal))
                first = lower[:, :, :].rearrange("p e f -> p (e f)").unsqueeze(1).to_broadcast([P, TB, E * E])
                eq3 = eq[:, :, :].rearrange("p (b e) f -> p b (e f)", b=TB)
                step(dve.tensor_tensor(eq3, eq3, first, ALU.mult))
                step(dve.tensor_tensor(gt[:, :, :], gt[:, :, :], eq[:, :, :], ALU.add))
                step(dve.tensor_reduce(r["rank"], gt[:, :, :], AX_X, ALU.add))
                step(dve.scalar_tensor_tensor(r["cw"], r["rank"], 2.0, r["s"], ALU.is_lt, ALU.mult))
                dve.wait_ge(s_cwone, f + 1)
                cw = R["cw"][:, :].rearrange("p (b e) -> p b e", b=TB)
                dve.tensor_copy(cw_rows[:, :, 0:E], cw)
                step(dve.tensor_copy(cw_rows[:, :, 32:32 + E], cw), wait=False)
                assert steps[0] == RT_DVE * (f + 1)
                dve.wait_ge(s_cwhi, f + 1)
                low = cwT[32:64, :]
                dve.tensor_tensor(low, ps[32:64, G_BANK:G_BANK + 2, :].rearrange("p a t -> p (a t)"),
                                  low.bitcast(F32), ALU.subtract).then_inc(s_cwT, 1)

                def lo(g):
                    dve.wait_ge(s_hhi, g + 1)
                    dve.tensor_tensor(hT_lo[:, g % HRING, :], ff_h[:, g % 2, :],
                                      hT_hi[:, g % HRING, :].bitcast(F32), ALU.subtract).then_inc(s_hlo, 1)

                def add_half(half):
                    dve.wait_ge(s_down, 2 * JT * f + JT * (half + 1))
                    for k in range(2):
                        rows = x[:, half * HB + 2 * k:half * HB + 2 * k + 2, :].rearrange("p b c -> p (b c)")
                        dve.scalar_tensor_tensor(rows, ps[:, ACC_BANK + k, :], 0.5, rows, ALU.mult, ALU.add)\
                            .then_inc(s_acc, 1)

                for u in range(2 * JT):
                    g = 2 * JT * f + u
                    dve.wait_ge(s_silu, g + 1)
                    dve.wait_ge(s_b, g + 1)
                    need(dve, s_h, g - 1)
                    dve.tensor_tensor(ff_m[:, g % 2, :], ps[:, B_BANK + g % 2, :], ff_s[:, g % 2, :], ALU.mult)\
                        .then_inc(s_m, 1)
                    dve.wait_ge(s_m, g + 1)
                    dve.wait_ge(s_g, g + 1)
                    need(dve, s_hlo, g - 1)
                    dve.tensor_tensor(ff_h[:, g % 2, :], ps[:, G_BANK + g % 2, :], ff_m[:, g % 2, :], ALU.mult)\
                        .then_inc(s_h, 1)
                    if u:
                        lo(g - 1)
                    if u == JT + 1:
                        add_half(0)
                lo(2 * JT * (f + 1) - 1)
                add_half(1)

            layer_norm(0)
            dve.wait_ge(s_in_b, 16)
            dve.tensor_copy(up_b[:, :, 0:J], stage_b).then_inc(s_cast_b, 1)
            ffn(0)
            dve.wait_ge(s_acc, 4)
            layer_norm(1)

            def bias_and_min(i, par, t):
                dve.wait_ge(s_scored, TB * i + t + 1)
                if t == 0:
                    dve.wait_ge(s_alibi, i + 1)
                u = t - 3
                need(dve, s_pt, NCH * i + FIRST[u] + len(CHUNKS[u]) if u >= 0
                     else NCH * (i - 1) + FIRST[TB + u] + len(CHUNKS[TB + u]))
                dve.memset(carrier[:, :], 0.0)
                k = P * (t + 1)
                dve.tensor_tensor_reduce(out=srow[:, P * ROW_AT[t]:P * ROW_AT[t] + k], in0=scores[:, 0:k], in1=alibi[:, par, T - k:T],
                                         scale=1.0, scalar=3e38, op0=ALU.add, op1=ALU.min,
                                         accum_out=neg_max[:, par, t:t + 1]).then_inc(s_ttr, 1)

            def pt_lo(i, t):
                for c, (b0, nb) in enumerate(CHUNKS[t]):
                    ch = NCH * i + FIRST[t] + c
                    dve.wait_ge(s_pthi, ch + 1)
                    dst = (slice(None), t % 2, slice(b0 * P, (b0 + nb) * P))
                    dve.tensor_tensor(pT_lo[dst], ps[:, PT_BANK + (FIRST[t] + c) % 2, 0:nb * P],
                                      pT_hi[dst].bitcast(F32), ALU.subtract).then_inc(s_ptlo, 1)

            def x_lo(use, dst, hi, scale):
                dve.wait_ge(s_xhi, use + 1)
                dve.scalar_tensor_tensor(dst, ps[:, X_BANK, :], scale[:, :], hi.bitcast(F32), ALU.mult, ALU.subtract)\
                    .then_inc(s_xlo, 1)

            def half_of(tile, par, half):
                return tile[:, par, half * HT:(half + 1) * HT]

            def qk_sum(n, half):
                dve.wait_ge(s_sq, 2 * n + half + 1)
                dve.tensor_reduce(qk_ss[:, half, :], sq[:, :, :].rearrange("p b (a d) -> p (b a) d", a=2), AX_X,
                                  ALU.add).then_inc(s_qkss, 1)

            def y_sum(h, par, half):
                dve.wait_ge(s_ysq, 2 * h + half + 1)
                dve.tensor_reduce(y_ss[:, half, :], ysq[:, :, :], AX_X, ALU.add).then_inc(s_yss, 1)
                sums = row_sum[:, par, half * HB:(half + 1) * HB]
                dve.scalar_tensor_tensor(y_e[:, half, :], sums, EPS, sums, ALU.mult, ALU.mult).then_inc(s_ye, 1)
                dve.wait_ge(s_yss, 2 * h + half + 1)
                dve.wait_ge(s_ye, 2 * h + half + 1)
                dve.scalar_tensor_tensor(y_t[:, half, :], y_ss[:, half, :], 1.0 / D, y_e[:, half, :],
                                         ALU.mult, ALU.add).then_inc(s_yt, 1)

            def add_projection(h, q):
                dve.wait_ge(s_pj, 4 * h + q + 1)
                rows = x[:, 2 * q:2 * q + 2, :].rearrange("p b c -> p (b c)")
                dve.tensor_tensor(rows, ps[:, M_BANK + q % 2, :], rows, ALU.add).then_inc(s_pjadd, 1)

            def body(i, it, par):
                att, nxt, prev, after = parts(i)
                n = i + 1
                for t in range(TB):
                    if att:
                        pt_lo(i, t)
                    if att and t < 2:
                        lo, hi, pos, scale = ((kT_lo, kT_hi, KB, k_scale), (qT_lo, qT_hi, QB, q_scale))[t]
                        x_lo(xuse(i, pos), half_of(lo, par, 1), half_of(hi, par, 1), scale)
                    if att and t < TB - 2:
                        bias_and_min(i, par, t + 2)
                    if nxt and t >= TB - 2:
                        bias_and_min(n, 1 - par, t - (TB - 2))
                    if prev and t == 1:
                        y_sum(i - 1, 1 - par, 1)
                    if nxt and t == 2:
                        qk_sum(n, 0)
                    if prev and t == 3:
                        x_lo(xuse(i, YB), yT_lo[:, 1, :], yT_hi[:, 1, :], y_scale)
                    if nxt and t == 4:
                        dve.wait_ge(s_vhi, n + 1)
                        dve.tensor_tensor(v_lo[:, 1 - par, :, :], qkv[:, :, 2 * D:3 * D],
                                          v_hi[:, 1 - par, :, :].bitcast(F32), ALU.subtract).then_inc(s_vlo, 1)
                        x_lo(xuse(i, KA), half_of(kT_lo, 1 - par, 0), half_of(kT_hi, 1 - par, 0), k_scale)
                        qk_sum(n, 1)
                    if nxt and t == 5:
                        x_lo(xuse(i, QA), half_of(qT_lo, 1 - par, 0), half_of(qT_hi, 1 - par, 0), q_scale)
                    if att and t == 5:
                        y_sum(i, par, 0)
                    if prev and t >= HB:
                        add_projection(i - 1, t - HB)
                    if att and t == 7:
                        x_lo(xuse(i, YA), yT_lo[:, 0, :], yT_hi[:, 0, :], y_scale)

            run_heads(dve, body)
            dve.wait_ge(s_pjadd, 4 * H)
            layer_norm(2)
            ffn(1)

        @block.tensor
        def _(pe):
            pe.wait_ge(s_const, 3)

            def layer_norm(k):
                for half in range(2):
                    pe.wait_ge(s_xn, TB * k + HB * (half + 1))
                    for c in range(CC):
                        for b in range(HB):
                            last = pe.transpose(ps[:, 2 * half + c, b * P:(b + 1) * P],
                                                xn[:, half * HB + b, c * P:(c + 1) * P], ident[:, :])
                        last.then_inc(s_xtr, 1)

            def ffn(f):
                pe.wait_ge(s_xTlo, 4 * (f * 2 + 1))
                pe.wait_ge(s_gw, 2)
                for tb in range(TB):
                    for n, (c, part) in enumerate((c, part) for c in range(CC) for part in (xT_hi, xT_lo)):
                        last = pe.matmul(ps[:, G_BANK, tb * 2 * E:(tb + 1) * 2 * E], part[:, c, tb * P:(tb + 1) * P],
                                         gw2[:, c, :], start=n == 0, stop=n == 3)
                last.then_inc(s_logit, 1)

                def product(bank, weights, jt, half):
                    for n, (c, part) in enumerate((c, part) for c in range(CC) for part in (xT_hi, xT_lo)):
                        last = pe.matmul(ps[:, bank, :], weights[:, c, jt * P:(jt + 1) * P],
                                         part[:, c, half * HT:(half + 1) * HT], start=n == 0, stop=n == 3)
                    return last

                def combine_rows():
                    pe.wait_ge(s_rt_dve, RT_DVE * (f + 1))
                    for tb in range(TB):
                        last = pe.transpose(ps[:, G_BANK + tb // HB, (tb % HB) * P:(tb % HB + 1) * P],
                                            cw_rows[:, tb, :], ident[:, :])
                    last.then_inc(s_cwtr, 1)
                    pe.wait_ge(s_expert, 16)
                    pe.wait_ge(s_cwT, f + 1)

                def up(g, half, jt):
                    if g == 0:
                        pe.wait_ge(s_cast_a, 1)
                        pe.wait_ge(s_cast_b, 1)
                    need(pe, s_silu, g - 1)
                    product(A_BANK + g % 2, up_a, jt, half).then_inc(s_a, 1)
                    need(pe, s_m, g - 1)
                    product(B_BANK + g % 2, up_b, jt, half).then_inc(s_b, 1)

                def spread(g, half, jt):
                    need(pe, s_h, g - 1)
                    pe.matmul(ps[:, G_BANK + g % 2, :], expert_of[:, jt * P:(jt + 1) * P],
                              cwT[:, half * HT:(half + 1) * HT], start=True, stop=True).then_inc(s_g, 1)

                def back(g, half, jt):
                    if g == 0:
                        pe.wait_ge(s_cast_d, 1)
                    if jt == 0:
                        need(pe, s_acc, 2 * (2 * f + half))
                    pe.wait_ge(s_hlo, g + 1)
                    for b in range(HB):
                        for part in (hT_hi, hT_lo):
                            last = pe.matmul(ps[:, ACC_BANK + b // 2, (b % 2) * C:(b % 2 + 1) * C],
                                             part[:, g % HRING, b * P:(b + 1) * P], down[:, jt, :],
                                             start=jt == 0 and part is hT_hi and b % 2 == 0,
                                             stop=jt == JT - 1 and part is hT_lo, skip_group_check=True)
                    last.then_inc(s_down, 1)

                units = [(2 * JT * f + JT * half + jt, half, jt) for half in range(2) for jt in range(JT)]
                for n, unit in enumerate(units):
                    up(*unit)
                    if n == 1:
                        combine_rows()
                        spread(*units[0])
                    if n:
                        spread(*unit)
                    if n >= 2:
                        back(*units[n - 2])
                back(*units[-2])
                back(*units[-1])

            layer_norm(0)
            ffn(0)
            layer_norm(1)
            pe.wait_ge(s_xTlo, 8)

            def score(i, par, t):
                if t == 0:
                    pe.wait_ge(s_xlo, xuse(i - 1, QA) + 1)
                if t == HB:
                    pe.wait_ge(s_xlo, xuse(i, QB) + 1)
                need(pe, s_ttr, TB * i + t)
                q = slice(t * P, (t + 1) * P)
                for c0 in range(0, t + 1, 4):
                    k = slice(c0 * P, min(t + 1, c0 + 4) * P)
                    for n, (a, b) in enumerate(((qT_hi, kT_hi), (qT_hi, kT_lo), (qT_lo, kT_hi))):
                        last = pe.matmul(scores[:, k], a[:, par, q], b[:, par, k], start=n == 0, stop=n == 2)
                last.then_inc(s_scored, 1)

            def project_qkv(n, tb):
                if tb == 0:
                    pe.wait_ge(s_wlo, n + 1)
                if tb < 2:
                    need(pe, s_pjadd, 4 * (n - 2) - 1 + tb)
                else:
                    need(pe, s_row, TB * n + tb - 1)
                last_of = 3 * CC - 1
                m = 0
                for c in range(CC):
                    for a, b in ((xT_hi, w_hi), (xT_hi, w_lo), (xT_lo, w_hi)):
                        last = pe.matmul(ps[:, M_BANK + tb % 2, 0:3 * D], a[:, c, tb * P:(tb + 1) * P], b[:, c, :],
                                         start=m == 0, stop=m == last_of)
                        m += 1
                last.then_inc(s_qkv, 1)

            def transpose_p(i, t):
                pe.wait_ge(s_exp, TB * i + t + 1)
                for c, (b0, nb) in enumerate(CHUNKS[t]):
                    need(pe, s_ptlo, NCH * i + FIRST[t] + c - 1)
                    for b in range(nb):
                        last = pe.transpose(ps[:, PT_BANK + (FIRST[t] + c) % 2, b * P:(b + 1) * P],
                                            srow[:, (ROW_AT[t] + b0 + b) * P:(ROW_AT[t] + b0 + b + 1) * P],
                                            ident[:, :])
                    last.then_inc(s_pt, 1)

            def values(i, par, t):
                if t == 0:
                    pe.wait_ge(s_vlo, i + 1)
                if t % HB == 0:
                    need(pe, s_yrow, 2 * i + t // HB)
                pe.wait_ge(s_ptlo, NCH * i + FIRST[t] + len(CHUNKS[t]))
                for s in range(t + 1):
                    blk = slice(s * P, (s + 1) * P)
                    for m, (a, b) in enumerate(((pT_hi, v_hi), (pT_hi, v_lo), (pT_lo, v_hi))):
                        last = pe.matmul(ps[:, Y_BANK, (t % HB) * D:(t % HB + 1) * D], a[:, t % 2, blk],
                                         b[:, par, s, :], start=s == 0 and m == 0, stop=s == t and m == 2)
                last.then_inc(s_pv, 1)

            def transpose_half(use, ready, count, blocks):
                pe.wait_ge(ready, count)
                need(pe, s_xlo, use)
                for b, block_ in enumerate(blocks):
                    last = pe.transpose(ps[:, X_BANK, b * P:(b + 1) * P], block_, ident[:, :])
                last.then_inc(s_xt, 1)

            def qk_blocks(half, which):
                return [qkv[:, half * HB + b, which * D:(which + 1) * D] for b in range(HB)]

            def y_blocks(half):
                return [yrow[:, half, b, :] for b in range(HB)]

            def project_y(h, q, use, rows):
                if q == 0:
                    pe.wait_ge(s_wplo, h + 1)
                if q % 2 == 0:
                    pe.wait_ge(s_xlo, use + 1)
                if q < 2:
                    need(pe, s_row, rows + q)
                else:
                    need(pe, s_pjadd, 4 * h + q - 1)
                for k in range(2):
                    b = (2 * q + k) % HB
                    for m, (a, w) in enumerate(((yT_hi, wp_hi), (yT_hi, wp_lo), (yT_lo, wp_hi))):
                        last = pe.matmul(ps[:, M_BANK + q % 2, k * C:(k + 1) * C], a[:, q // 2, b * P:(b + 1) * P], w[:, :],
                                         start=m == 0, stop=m == 2)
                last.then_inc(s_pj, 1)

            def body(i, it, par):
                att, nxt, prev, after = parts(i)
                n = i + 1
                for t in range(TB):
                    if att:
                        transpose_p(i, t)
                    if att and t < 2:
                        transpose_half(xuse(i, (KB, QB)[t]), s_qkn, 2 * i + 2, qk_blocks(1, 1 - t))
                    if att and t < TB - 2:
                        score(i, par, t + 2)
                    if nxt and t < HB:
                        project_qkv(n, 2 * t)
                    if prev and t == 0:
                        values(i - 1, 1 - par, TB - 1)
                    if att and t > 0:
                        values(i, par, t - 1)
                    if nxt and t < HB:
                        project_qkv(n, 2 * t + 1)
                    if nxt and t >= TB - 2:
                        score(n, 1 - par, t - (TB - 2))
                    if prev and t == 3:
                        transpose_half(xuse(i, YB), s_yn, 2 * i, y_blocks(1))
                    if nxt and t in (4, 5):
                        transpose_half(xuse(i, (KA, QA)[t - 4]), s_qkn, 2 * n + 1, qk_blocks(0, 5 - t))
                    if prev and t >= HB:
                        project_y(i - 1, t - HB, xuse(i - 1, YA) if t < 6 else xuse(i, YB),
                                  TB * n + 7 if nxt else TB * H - 1)
                    if att and t == 7:
                        transpose_half(xuse(i, YA), s_yn, 2 * i + 1, y_blocks(0))

            run_heads(pe, body)
            layer_norm(2)
            ffn(1)


def kernel(**inputs):
    import concourse.bacc as bacc
    from concourse.bass_utils import run_bass_kernel_spmd

    g = {k.removeprefix("L0_"): np.asarray(v) for k, v in inputs.items()}
    x = g["attn_x"]
    _, T, C = x.shape
    H, D = 16, P
    E = g["ffn_gate_w"].shape[0]

    def heads(w):
        return w.reshape(C // P, P, H, D).transpose(2, 1, 0, 3)

    def columns(w, shared):
        return np.concatenate([w.reshape(-1, C), shared], axis=0).T

    arrays = {
        "x_in": x.reshape(T, C),
        "w_qkv": np.concatenate([heads(g["attn_Wq"]), heads(g["attn_Wk"]), heads(g["attn_Wv"])], axis=3),
        "w_proj": g["attn_Wproj"].reshape(H, D, C),
        "q_w": g["attn_q_rms_w"].reshape(D, 1),
        "k_w": g["attn_k_rms_w"].reshape(D, 1),
        "y_w": g["attn_subln_w"].reshape(D, 1),
        "gate_w": g["ffn_gate_w"].T,
        "gate_b": np.tile(g["ffn_gate_b"], (P, T // P)),
        "w_up_a": columns(g["ffn_w1"], g["ffn_sw1"]),
        "w_up_b": columns(g["ffn_w3"], g["ffn_sw3"]),
        "w_down": np.concatenate([g["ffn_w2"].transpose(0, 2, 1).reshape(-1, C), g["ffn_sw2"].T], axis=0),
    }
    arrays = {k: np.ascontiguousarray(v) for k, v in arrays.items()}
    nc = bacc.Bacc("TRN2", target_bir_lowering=False, num_devices=1)
    aps = [nc.dram_tensor(k, v.shape, mybir.dt.from_np(v.dtype), kind="ExternalInput").ap() for k, v in arrays.items()]
    out = nc.dram_tensor("out", (T, C), F32, kind="ExternalOutput").ap()
    macaron_kernel(nc, *aps, out)
    result = run_bass_kernel_spmd(nc, [arrays], core_ids=[0])
    return result.results[0]["out"].reshape(x.shape)
```

```python
from contextlib import ExitStack

import numpy as np

import concourse.bass as bass
from concourse import mybir

F32 = mybir.dt.float32
F32R = mybir.dt.float32r
BF16 = mybir.dt.bfloat16
ALU = mybir.AluOpType
ACT = mybir.ActivationFunctionType
AX_X = mybir.AxisListType.X

P = 128
EPS = 1e-5
MASKED = 1e30
LN_FLOOR = 60
BANK = 512


def need(engine, semaphore, count):
    if not isinstance(count, int) or count > 0:
        engine.wait_ge(semaphore, count)


def macaron_kernel(nc, x_in, w_qkv, w_proj, q_w, k_w, y_w, gate_w, gate_b, w_up_a, w_up_b, w_down, out):
    T, C = x_in.shape
    H = w_qkv.shape[0]
    D = P
    E = gate_w.shape[1]
    J = w_down.shape[0]
    INTER = J // (E + 1)
    TB = T // P
    CC = C // P
    JT = -(-J // P)
    JPAD = JT * P
    JTAIL = J - (JT - 1) * P
    HB = TB // 2
    HT = T // 2
    assert (T, C, D) == (1024, 256, 128) and HT == BANK

    SLOPE = [2.0 ** (-8.0 / H * (h + 1)) for h in range(2)]
    SLOPE_STEP = 2.0 ** (-8.0 / H * 2)
    QSCALE = -float(D) ** -0.5

    CHUNKS = [[(c, min(4, t + 1 - c)) for c in range(0, t + 1, 4)] for t in range(TB)]
    FIRST = [sum(len(CHUNKS[u]) for u in range(t)) for t in range(TB)]
    NCH = sum(len(c) for c in CHUNKS)

    with ExitStack() as ctx:
        def sb(name, shape, dt=F32):
            return ctx.enter_context(nc.sbuf_tensor(name, shape, dt))

        def sem(name):
            return ctx.enter_context(nc.semaphore(name))

        x = sb("x", [P, TB, C])
        xT_hi = sb("xT_hi", [P, CC, T], F32R)
        xT_lo = sb("xT_lo", [P, CC, T], F32R)
        ident = sb("ident", [P, P])
        ROW_AT = [18, 12, 15, 8, 0, 15, 8, 0]
        srow = sb("srow", [P, 21 * P])
        xn = srow[:, 0:TB * C].rearrange("p (b c) -> p b c", c=C)
        stage_a = srow[:, 0:TB * C].bitcast(BF16)[:, 0:CC * J].rearrange("p (c j) -> p c j", c=CC)
        PAIR_AT = [8, 0, 8, 0]
        pT_hi = sb("pT_hi", [P, 14, 2 * P], F32R)
        pT_lo = sb("pT_lo", [P, 14, 2 * P], F32R)
        qkv = sb("qkv", [P, TB, 3 * D])
        sq = sb("sq", [P, HB, 2 * D])
        qT_hi = sb("qT_hi", [P, 2, T], F32R)
        qT_lo = sb("qT_lo", [P, 2, T], F32R)
        kT = sb("kT", [P, 2, 2, T], F32R)
        kT_hi, kT_lo = kT[:, 0, :, :], kT[:, 1, :, :]
        v_hi = sb("v_hi", [P, 2, TB, D], F32R)
        v_lo = sb("v_lo", [P, 2, TB, D], F32R)
        raw = sb("raw", [P, 2 * (CC * 3 * D + C)])
        wraw = raw[:, 0:2 * CC * 3 * D].rearrange("p (a c d) -> p a c d", a=2, c=CC)
        wpraw = raw[:, 2 * CC * 3 * D:].rearrange("p (a c) -> p a c", a=2)
        stage_d = raw[:, :].bitcast(BF16)[:, 0:JT * C].rearrange("p (t c) -> p t c", t=JT)
        w_hi = sb("w_hi", [P, CC, 3 * D], F32R)
        w_lo = sb("w_lo", [P, CC, 3 * D], F32R)
        wp_hi = sb("wp_hi", [P, C], F32R)
        wp_lo = sb("wp_lo", [P, C], F32R)
        alibi = sb("alibi", [P, 2, T])
        stage_b = alibi[:, :, :].rearrange("p a t -> p (a t)").bitcast(BF16)[:, 0:CC * J].rearrange(
            "p (c j) -> p c j", c=CC)
        yT_hi = sb("yT_hi", [P, T], F32R)
        yT_lo = sb("yT_lo", [P, T], F32R)
        ysq = sb("ysq", [P, T])
        up_a = sb("up_a", [P, CC, JPAD], F32R)
        up_b = sb("up_b", [P, CC, JPAD], F32R)
        down = kT[:, :, :, :].rearrange("p a b t -> p (a b t)")[:, 0:JT * C].rearrange("p (t c) -> p t c", t=JT)
        expert_of = sb("expert_of", [P, JPAD], F32R)
        cwT = qT_hi[:, 0, :]
        gt, eq = (ysq[:, k * TB * E * E:(k + 1) * TB * E * E].rearrange("p (b f) -> p b f", f=E) for k in range(2))
        flat = qkv[:, :, :].rearrange("p b d -> p (b d)")
        ff_s = flat[:, 0:2 * BANK].rearrange("p (r t) -> p r t", r=2)
        ff_m = flat[:, 2 * BANK:4 * BANK].rearrange("p (r t) -> p r t", r=2)
        ff_h = flat[:, 4 * BANK:6 * BANK].rearrange("p (r t) -> p r t", r=2)
        HRING = 3
        hT_hi, hT_lo = (t[:, 0:2 * HRING, :].rearrange("p a t -> p (a t)").rearrange("p (r t) -> p r t", t=BANK)
                        for t in (pT_hi, pT_lo))
        cw_rows = sq[:, :, :].rearrange("p a (r e) -> p (a r) e", e=P)
        expert_f = ysq

        bn = sb("bn", [P, TB, 6])
        mv = sb("mv", [P, TB, 2])
        lnv = sb("lnv", [P, TB])
        rstd = sb("rstd", [P, TB])
        qk_ss = sb("qk_ss", [P, 2, HB * 2])
        qk_ln = sb("qk_ln", [P, 2, HB * 2])
        qk_r = sb("qk_r", [P, 2, HB * 2])
        y_e = sb("y_e", [P, TB])
        y_t = sb("y_t", [P, TB])
        y_ln = sb("y_ln", [P, TB])
        y_f = sb("y_f", [P, TB])
        ones = sb("ones", [P, 1])
        neg_max = sb("neg_max", [P, 2, TB])
        row_sum = sb("row_sum", [P, 2, TB])
        q_w_sb = sb("q_w_sb", [P, 1])
        q_scale = sb("q_scale", [P, 1])
        k_scale = sb("k_scale", [P, 1])
        y_scale = sb("y_scale", [P, 1])
        epst = sb("epst", [P, 1])
        slope_step = sb("slope_step", [P, 1])
        carrier = sb("carrier", [P, 1])
        gw = sb("gw", [P, CC, E])
        gw2 = sb("gw2", [P, CC, 2 * E], F32R)
        gb = sb("gb", [P, TB * E])
        lower = sb("lower", [P, E, E])
        R = {n: sb("r_" + n, [P, TB * E]) for n in
             ("z", "a", "u", "w", "lw", "d", "i", "rd", "v", "sp", "L", "mn", "s", "b")}
        R |= {"rank": R["d"], "cw": R["w"]}

        ps = ctx.enter_context(nc.psum_tensor("ps", [P, 8, BANK], F32))
        PT_BANK, M_BANK = 2, 4
        Y_BANK = (7, 6)
        X_BANK = (6, 7)
        A_BANK, B_BANK, G_BANK, ACC_BANK = 0, 2, 4, 6
        scores = ps[:, 0:2, :].rearrange("p a t -> p (a t)")
        y_sums = ps[:, X_BANK[0], 0:TB]

        s_x = [sem(f"s_x{i}") for i in range(2)]
        s_small = sem("s_small")
        s_in_a, s_in_b, s_in_d = sem("s_in_a"), sem("s_in_b"), sem("s_in_d")
        s_w = [sem(f"s_w{i}") for i in range(2)]
        s_wp = [sem(f"s_wp{i}") for i in range(2)]
        s_expert = sem("s_expert")
        s_out = sem("s_out")
        s_zeroed, s_const = sem("s_zeroed"), sem("s_const")
        s_cwzero, s_cwone = sem("s_cwzero"), sem("s_cwone")
        s_escratch, s_eof, s_dist, s_cast_d = sem("s_escratch"), sem("s_eof"), sem("s_dist"), sem("s_cast_d")
        s_alibi = sem("s_alibi")
        s_sq, s_qkn = sem("s_sq"), sem("s_qkn")
        s_wlo, s_wplo, s_vlo = sem("s_wlo"), sem("s_wplo"), sem("s_vlo")
        s_cast_a = sem("s_cast_a")
        s_lnv, s_rstd, s_xThi = sem("s_lnv"), sem("s_rstd"), sem("s_xThi")
        s_rt_act, s_cwhi = sem("s_rt_act"), sem("s_cwhi")
        s_silu, s_hhi = sem("s_silu"), sem("s_hhi")
        s_exp, s_pthi, s_row = sem("s_exp"), sem("s_pthi"), sem("s_row")
        s_qkln, s_qkr, s_xhi, s_vhi = sem("s_qkln"), sem("s_qkr"), sem("s_xhi"), sem("s_vhi")
        s_yhi, s_ysq, s_yln, s_yf = sem("s_yhi"), sem("s_ysq"), sem("s_yln"), sem("s_yf")
        s_whi, s_wphi = sem("s_whi"), sem("s_wphi")
        s_cast_b, s_gw, s_qs = sem("s_cast_b"), sem("s_gw"), sem("s_qs")
        s_bn, s_mv, s_xn, s_xTlo = sem("s_bn"), sem("s_mv"), sem("s_xn"), sem("s_xTlo")
        s_rt_dve, s_cwT = sem("s_rt_dve"), sem("s_cwT")
        s_m, s_h, s_hlo, s_acc = sem("s_m"), sem("s_h"), sem("s_hlo"), sem("s_acc")
        s_ttr, s_ptlo, s_qkss, s_xlo = sem("s_ttr"), sem("s_ptlo"), sem("s_qkss"), sem("s_xlo")
        s_ylo, s_ye, s_yt, s_pjadd = sem("s_ylo"), sem("s_ye"), sem("s_yt"), sem("s_pjadd")
        s_xtr, s_logit, s_cwtr = sem("s_xtr"), sem("s_logit"), sem("s_cwtr")
        s_a, s_b, s_g, s_down = sem("s_a"), sem("s_b"), sem("s_g"), sem("s_down")
        s_scored, s_pt, s_pv, s_qkv = sem("s_scored"), sem("s_pt"), sem("s_pv"), sem("s_qkv")
        s_xt, s_pj, s_yss = sem("s_xt"), sem("s_pj"), sem("s_yss")

        RT_DVE, RT_ACT = 22, 5

        block = ctx.enter_context(nc.Block())

        KB, QB, KA, QA = range(4)

        def xuse(i, pos):
            return 2 + 4 * i + pos

        def pair_part(pT, t, b0, nb):
            at = PAIR_AT[t // 2] + b0
            return pT[:, at:at + nb, (t % 2) * P:(t % 2 + 1) * P]

        def chunk_bank(t, c, nb):
            return ps[:, PT_BANK + (FIRST[t] + c) % 2, 0:nb * P].rearrange("p (b k) -> p b k", k=P)

        def half_columns(half):
            return slice(half * HT, (half + 1) * HT)

        def run_heads(engine, body):
            for i in (-1, 0, 1):
                body(i, i // 2, i % 2)
            with engine.Fori(1, H // 2 - 1) as it:
                body(2 * it, it, 0)
                body(2 * it + 1, it, 1)
            for i in (H - 2, H - 1, H):
                body(i, i // 2, i % 2)

        def parts(i):
            if not isinstance(i, int):
                return True, True, True, True
            return 0 <= i < H, i + 1 < H, i >= 1, i + 2 < H

        @block.sync
        def _(sp):
            def load_down():
                sp.dma_start(stage_d[:, 0:JT - 1, :],
                             w_down[0:(JT - 1) * P, :].rearrange("(t p) c -> p t c", p=P)).then_inc(s_in_d, 16)

            def load_down_tail():
                sp.dma_start(stage_d[0:JTAIL, JT - 1, :], w_down[(JT - 1) * P:, :]).then_inc(s_in_d, 16)

            sp.dma_start(x[:, 0:HB, :], x_in[0:HT, :].rearrange("(b p) c -> p b c", p=P)).then_inc(s_x[0], 16)
            sp.dma_start(x[:, HB:, :], x_in[HT:, :].rearrange("(b p) c -> p b c", p=P)).then_inc(s_x[1], 16)
            for dst, src in ((gw[:, :, :], gate_w.rearrange("(c p) e -> p c e", p=P)), (gb[:, :], gate_b),
                             (q_w_sb[:, :], q_w), (k_scale[:, :], k_w), (y_scale[:, :], y_w)):
                sp.dma_start(dst, src).then_inc(s_small, 16)
            sp.dma_start(stage_b, w_up_b.rearrange("(c p) j -> p c j", p=P)).then_inc(s_in_b, 16)
            load_down()
            sp.wait_ge(s_zeroed, 3)
            load_down_tail()
            sp.wait_ge(s_xtr, 4)
            sp.dma_start(stage_a, w_up_a.rearrange("(c p) j -> p c j", p=P)).then_inc(s_in_a, 16)

            sp.wait_ge(s_eof, 2)
            sp.dma_start(expert_of[32:32 + E + 1, :].bitcast(F32), expert_of[0:E + 1, :].bitcast(F32)).then_inc(s_expert, 16)

            def load_w(n, slot):
                need(sp, s_wlo, n - 1)
                sp.dma_start(wraw[:, slot, :, :], w_qkv[n, :, :, :]).then_inc(s_w[slot], 16)

            def load_wp(n, slot):
                need(sp, s_wplo, n - 1)
                sp.dma_start(wpraw[:, slot, :], w_proj[n, :, :]).then_inc(s_wp[slot], 16)

            sp.wait_ge(s_cast_d, 1)
            for n in range(2):
                load_w(n, n)
                load_wp(n, n)
            for n in (2, 3):
                load_w(n, n % 2)
            with sp.Fori(2, H // 2) as it:
                for slot in range(2):
                    load_w(2 * it + slot, slot)
                    load_wp(2 * it + slot - 2, slot)
            for n in (H - 2, H - 1):
                load_wp(n, n % 2)
            sp.wait_ge(s_zeroed, 4)
            load_down()
            load_down_tail()
            for half in range(2):
                sp.wait_ge(s_acc, 2 * 3 + 2 * half)
                sp.dma_start(out[half * HT:(half + 1) * HT, :].rearrange("(b p) c -> p b c", p=P),
                             x[:, half * HB:(half + 1) * HB, :]).then_inc(s_out, 16)
            sp.wait_ge(s_out, 32)

        @block.gpsimd
        def _(pool):
            pool.memset(ident[:, :], 0.0).then_inc(s_zeroed, 1)
            pool.wait_ge(s_zeroed, 1)
            pool.affine_select(out=ident[:, :], in_=ident[:, :], compare_op=ALU.not_equal, fill=1.0, base=0,
                               pattern=[[-1, P]], channel_multiplier=1).then_inc(s_const, 1)
            pool.memset(epst[:, :], EPS).then_inc(s_const, 1)
            pool.memset(slope_step[:, :], SLOPE_STEP)
            pool.memset(ones[:, :], 1.0)
            pool.memset(lower[:, :, :], 1.0).then_inc(s_zeroed, 1)
            pool.wait_ge(s_zeroed, 2)
            pool.affine_select(out=lower[:, :, :], in_=lower[:, :, :], compare_op=ALU.is_gt, fill=0.0, base=0,
                               pattern=[[1, E], [-1, E]], channel_multiplier=0).then_inc(s_const, 1)
            pool.memset(up_a[:, :, J:JPAD].bitcast(F32), 0.0)
            pool.memset(up_b[:, :, J:JPAD].bitcast(F32), 0.0)
            pool.memset(stage_d[:, JT - 1, :], 0.0).then_inc(s_zeroed, 1)

            def clear_combine_rows(f):
                need(pool, s_qkss, 2 * H * f)
                pool.memset(cw_rows[:, :, :], 0.0).then_inc(s_cwzero, 1)
                pool.wait_ge(s_cwzero, f + 1)
                for r in (0, 32):
                    last = pool.memset(cw_rows[:, :, r + E:r + E + 1], 1.0)
                last.then_inc(s_cwone, 1)

            clear_combine_rows(0)
            for n, lo in enumerate(range(0, JPAD, T)):
                k = min(T, JPAD - lo)
                need(pool, s_eof, n)
                pool.memset(expert_f[:, 0:k], 1.0).then_inc(s_escratch, 1)
                pool.wait_ge(s_escratch, 2 * n + 1)
                pool.affine_select(out=expert_f[:, 0:k], in_=expert_f[:, 0:k], compare_op=ALU.is_ge, fill=0.0,
                                   base=lo, pattern=[[1, k]], channel_multiplier=-INTER).then_inc(s_escratch, 1)
                pool.wait_ge(s_escratch, 2 * n + 2)
                pool.affine_select(out=expert_of[:, lo:lo + k], in_=expert_f[:, 0:k], compare_op=ALU.is_ge, fill=0.0,
                                   base=INTER - 1 - lo, pattern=[[-1, k]], channel_multiplier=INTER).then_inc(s_eof, 1)
            pool.wait_ge(s_in_d, 32)
            pool.tensor_copy(down[:, :, :], stage_d[:, :, :]).then_inc(s_cast_d, 1)
            pool.wait_ge(s_cast_b, 1)
            dist = alibi[:, 1, :]
            pool.iota(dist, pattern=[[-1, T]], base=T - P, channel_multiplier=1,
                      allow_small_or_imprecise_dtypes=True).then_inc(s_dist, 1)
            pool.wait_ge(s_dist, 1)
            pool.affine_select(out=dist, in_=dist, compare_op=ALU.is_ge, fill=MASKED, base=T - P,
                               pattern=[[-1, T]], channel_multiplier=1).then_inc(s_dist, 1)
            pool.wait_ge(s_dist, 2)
            pool.tensor_scalar(alibi[:, 0, :], dist, SLOPE[0], None, ALU.mult).then_inc(s_alibi, 1)
            pool.tensor_scalar(dist, dist, SLOPE[1], None, ALU.mult).then_inc(s_alibi, 1)

            def split_w(n, slot):
                pool.wait_ge(s_whi, n + 1)
                pool.tensor_tensor(w_lo[:, :, :], wraw[:, slot, :, :], w_hi[:, :, :].bitcast(F32), ALU.subtract)\
                    .then_inc(s_wlo, 1)

            def square_qk(n, half):
                pool.wait_ge(s_row, TB * n + HB * (half + 1))
                need(pool, s_qkss, 2 * n + half)
                qk = qkv[:, half * HB:(half + 1) * HB, 0:2 * D]
                pool.tensor_tensor(sq[:, :, :], qk, qk, ALU.mult).then_inc(s_sq, 1)

            def scale_qk(n, half):
                pool.wait_ge(s_qkr, 2 * n + half + 1)
                qk = qkv[:, half * HB:(half + 1) * HB, 0:2 * D].rearrange("p b (a d) -> p b a d", a=2)
                r = qk_r[:, half, :].rearrange("p (b a) -> p b a", a=2).unsqueeze(3).to_broadcast([P, HB, 2, D])
                pool.tensor_tensor(qk, qk, r, ALU.mult).then_inc(s_qkn, 1)

            split_w(0, 0)
            step_t = slope_step[:, :]

            def body(i, it, par):
                att, nxt, prev, after = parts(i)
                n = i + 1
                if prev and nxt:
                    pool.wait_ge(s_ttr, TB * i)
                    pool.tensor_tensor(alibi[:, 1 - par, :], alibi[:, 1 - par, :], step_t.to_broadcast([P, T]), ALU.mult)\
                        .then_inc(s_alibi, 1)
                if nxt:
                    square_qk(n, 0)
                if prev:
                    pool.wait_ge(s_wphi, i)
                    pool.tensor_tensor(wp_lo[:, :], wpraw[:, 1 - par, :], wp_hi[:, :].bitcast(F32), ALU.subtract)\
                        .then_inc(s_wplo, 1)
                if nxt:
                    scale_qk(n, 0)
                    square_qk(n, 1)
                    pool.wait_ge(s_vhi, n + 1)
                    pool.tensor_tensor(v_lo[:, 1 - par, :, :], qkv[:, :, 2 * D:3 * D],
                                       v_hi[:, 1 - par, :, :].bitcast(F32), ALU.subtract).then_inc(s_vlo, 1)
                if after:
                    split_w(i + 2, par)
                if nxt:
                    scale_qk(n, 1)

            run_heads(pool, body)
            pool.wait_ge(s_wlo, H)
            pool.wait_ge(s_wplo, H)
            pool.memset(stage_d[:, JT - 1, :], 0.0).then_inc(s_zeroed, 1)
            clear_combine_rows(1)
            pool.wait_ge(s_scored, TB * H)
            pool.wait_ge(s_in_d, 64)
            pool.tensor_copy(down[:, :, :], stage_d[:, :, :]).then_inc(s_cast_d, 1)

        @block.scalar
        def _(act):
            def layer_norm(k):
                act.wait_ge(s_mv, k + 1)
                act.activation(lnv[:, :], mv[:, :, 1], ACT.Ln, bias=epst[:, :]).then_inc(s_lnv, 1)
                act.wait_ge(s_lnv, k + 1)
                act.activation(rstd[:, :], lnv[:, :], ACT.Exp, scale=-0.5).then_inc(s_rstd, 1)
                for half in range(2):
                    for c in range(CC):
                        act.wait_ge(s_xtr, 4 * k + 2 * half + c + 1)
                        act.activation(xT_hi[:, c, half * HT:(half + 1) * HT], ps[:, 2 * half + c, :], ACT.Copy)\
                            .then_inc(s_xThi, 1)

            def ffn(f):
                base = RT_DVE * f
                for n, (name, src, func, scale, after_dve) in enumerate((
                        ("a", "z", ACT.Abs, 1.0, 2), ("u", "a", ACT.Exp, -1.0, 2), ("lw", "w", ACT.Ln, 1.0, 3),
                        ("L", "sp", ACT.Ln, 1.0, 12), ("s", "L", ACT.Exp, 0.5, 14))):
                    act.wait_ge(s_rt_dve, base + after_dve)
                    if n == 1:
                        act.wait_ge(s_rt_act, RT_ACT * f + 1)
                    act.activation(R[name][:, :], R[src][:, :], func, scale=scale).then_inc(s_rt_act, 1)
                act.preload_act_table_set("silu_and_others")
                act.wait_ge(s_cwtr, f + 1)
                act.activation(cwT[:, :], ps[:, G_BANK:G_BANK + 2, :].rearrange("p a t -> p (a t)"), ACT.Copy)\
                    .then_inc(s_cwhi, 1)

                def hi(g):
                    act.wait_ge(s_h, g + 1)
                    need(act, s_down, g - HRING + 1)
                    act.activation(hT_hi[:, g % HRING, :], ff_h[:, g % 2, :], ACT.Copy).then_inc(s_hhi, 1)

                for u in range(2 * JT):
                    g = 2 * JT * f + u
                    act.wait_ge(s_a, g + 1)
                    need(act, s_m, g - 1)
                    act.activation(ff_s[:, g % 2, :], ps[:, A_BANK + g % 2, :], ACT.Silu).then_inc(s_silu, 1)
                    if u:
                        hi(g - 1)
                hi(2 * JT * (f + 1) - 1)

            act.preload_act_table_set("natural_log_exp_and_others")
            layer_norm(0)
            act.wait_ge(s_in_a, 16)
            act.activation(up_a[:, :, 0:J], stage_a, ACT.Copy).then_inc(s_cast_a, 1)
            ffn(0)
            act.preload_act_table_set("natural_log_exp_and_others")
            layer_norm(1)

            def split_w(n, slot, use):
                act.wait_ge(s_w[slot], 16 * (use + 1))
                need(act, s_qkv, TB * n)
                act.activation(w_hi[:, :, :], wraw[:, slot, :, :], ACT.Copy).then_inc(s_whi, 1)

            def exp(i, par, t):
                act.wait_ge(s_ttr, TB * i + t + 1)
                row = srow[:, P * ROW_AT[t]:P * (ROW_AT[t] + t + 1)]
                act.activation(row, row, ACT.Exp, bias=neg_max[:, par, t:t + 1], scale=-1.0,
                               accum_out=row_sum[:, par, t:t + 1]).then_inc(s_exp, 1)

            def qkv_row(n, tb):
                act.wait_ge(s_qkv, TB * n + tb + 1)
                if tb == 0:
                    need(act, s_vlo, n)
                act.activation(qkv[:, tb, :], ps[:, M_BANK + tb % 2, 0:3 * D], ACT.Copy).then_inc(s_row, 1)

            def pt_hi(i, t):
                for c, (b0, nb) in enumerate(CHUNKS[t]):
                    ch = NCH * i + FIRST[t] + c
                    act.wait_ge(s_pt, ch + 1)
                    act.activation(pair_part(pT_hi, t, b0, nb), chunk_bank(t, c, nb), ACT.Copy).then_inc(s_pthi, 1)

            def x_hi(use, half, dst, scale):
                act.wait_ge(s_xt, use + 1)
                act.activation(dst, ps[:, X_BANK[half], :], ACT.Copy, scale=scale[:, :]).then_inc(s_xhi, 1)

            def half_of(tile, par, half):
                return tile[:, par, half * HT:(half + 1) * HT]

            def qk_rsqrt(n, half):
                act.wait_ge(s_qkss, 2 * n + half + 1)
                act.activation(qk_ln[:, half, :], qk_ss[:, half, :], ACT.Ln, scale=1.0 / D, bias=epst[:, :])\
                    .then_inc(s_qkln, 1)
                act.wait_ge(s_qkln, 2 * n + half + 1)
                act.activation(qk_r[:, half, :], qk_ln[:, half, :], ACT.Exp, scale=-0.5).then_inc(s_qkr, 1)

            def y_hi(h, half):
                act.wait_ge(s_pv, 2 * h + half + 1)
                need(act, s_pj, 4 * (h - 1) + 2 * half + 2)
                act.activation(yT_hi[:, half_columns(half)], ps[:, Y_BANK[half], :], ACT.Copy, scale=y_scale[:, :])\
                    .then_inc(s_yhi, 1)
                need(act, s_yss, h)
                act.activation(ysq[:, half_columns(half)], ps[:, Y_BANK[half], :], ACT.Square).then_inc(s_ysq, 1)

            def y_rsqrt(h):
                act.wait_ge(s_yt, h + 1)
                act.activation(y_ln[:, :], y_t[:, :], ACT.Ln).then_inc(s_yln, 1)
                act.wait_ge(s_yln, h + 1)
                act.activation(y_f[:, :], y_ln[:, :], ACT.Exp, scale=-0.5).then_inc(s_yf, 1)

            split_w(0, 0, 0)
            act.wait_ge(s_qs, 1)

            def body(i, it, par):
                att, nxt, prev, after = parts(i)
                n = i + 1
                for t in range(TB):
                    if att:
                        pt_hi(i, t)
                    if nxt and t < HB:
                        qkv_row(n, 2 * t)
                    if att and t < 2:
                        dst, pos, scale = ((kT_hi, KB, k_scale), (qT_hi, QB, q_scale))[t]
                        x_hi(xuse(i, pos), 1, half_of(dst, par, 1), scale)
                    if nxt and t in (4, 5):
                        dst, pos, scale = ((kT_hi, KA, k_scale), (qT_hi, QA, q_scale))[t - 4]
                        x_hi(xuse(i, pos), 0, half_of(dst, 1 - par, 0), scale)
                    if nxt and t == 4:
                        act.wait_ge(s_row, TB * (n + 1))
                        act.activation(v_hi[:, 1 - par, :, :], qkv[:, :, 2 * D:3 * D], ACT.Copy).then_inc(s_vhi, 1)
                    if nxt and t == 6:
                        qk_rsqrt(n, 1)
                    if after and t == 5:
                        split_w(i + 2, par, it + 1)
                    if att and t < TB - 2:
                        exp(i, par, t + 2)
                    if nxt and t < HB:
                        qkv_row(n, 2 * t + 1)
                    if att and t == 7:
                        y_hi(i, 0)
                    if nxt and t >= TB - 2:
                        exp(n, 1 - par, t - (TB - 2))
                    if prev and t == 1:
                        wp_use = it - 1 + (par + 1) // 2
                        act.wait_ge(s_wp[1 - par], 16 * (wp_use + 1))
                        need(act, s_pj, 4 * (i - 1))
                        act.activation(wp_hi[:, :], wpraw[:, 1 - par, :], ACT.Copy).then_inc(s_wphi, 1)
                    if nxt and t == 2:
                        qk_rsqrt(n, 0)
                    if prev and t == 2:
                        y_hi(i - 1, 1)
                    if prev and t == 3:
                        y_rsqrt(i - 1)

            run_heads(act, body)
            layer_norm(2)
            ffn(1)

        @block.vector
        def _(dve):
            dve.wait_ge(s_const, 3)
            dve.wait_ge(s_small, 80)
            dve.tensor_copy(gw2[:, :, 0:E], gw[:, :, :]).then_inc(s_gw, 1)
            dve.tensor_scalar(q_scale[:, :], q_w_sb[:, :], QSCALE, None, ALU.mult).then_inc(s_qs, 1)
            dve.wait_ge(s_gw, 1)
            dve.tensor_tensor(gw2[:, :, E:2 * E], gw[:, :, :], gw2[:, :, 0:E].bitcast(F32), ALU.subtract)\
                .then_inc(s_gw, 1)

            def layer_norm(k):
                for tb in range(TB):
                    if k == 0 and tb % HB == 0:
                        dve.wait_ge(s_x[tb // HB], 16)
                    last = dve.bn_stats(bn[:, tb, :], x[:, tb, :])
                last.then_inc(s_bn, 1)
                dve.wait_ge(s_bn, k + 1)
                for tb in range(TB):
                    last = dve.bn_aggr(mv[:, tb, :], bn[:, tb, :])
                last.then_inc(s_mv, 1)
                dve.wait_ge(s_rstd, k + 1)
                for tb in range(TB):
                    dve.tensor_scalar(xn[:, tb, :], x[:, tb, :], mv[:, tb, 0:1], rstd[:, tb:tb + 1],
                                      ALU.subtract, ALU.mult).then_inc(s_xn, 1)
                for half in range(2):
                    for c in range(CC):
                        dve.wait_ge(s_xThi, 4 * k + 2 * half + c + 1)
                        dst = (slice(None), c, slice(half * HT, (half + 1) * HT))
                        dve.tensor_tensor(xT_lo[dst], ps[:, 2 * half + c, :], xT_hi[dst].bitcast(F32), ALU.subtract)\
                            .then_inc(s_xTlo, 1)

            def ffn(f):
                steps = [RT_DVE * f]

                def step(instruction, wait=True):
                    instruction.then_inc(s_rt_dve, 1)
                    steps[0] += 1
                    if wait:
                        dve.wait_ge(s_rt_dve, steps[0])

                def after_act(n):
                    dve.wait_ge(s_rt_act, RT_ACT * f + n)

                r = {name: tile[:, :] for name, tile in R.items()}
                logits = ps[:, G_BANK, 0:TB * 2 * E].rearrange("p (b e) -> p b e", b=TB)
                by_block = R["v"][:, :].rearrange("p (b e) -> p b e", b=TB)
                dve.wait_ge(s_logit, f + 1)
                step(dve.tensor_copy(by_block, logits[:, :, E:2 * E]))
                step(dve.tensor_tensor(R["z"][:, :].rearrange("p (b e) -> p b e", b=TB), logits[:, :, 0:E],
                                       by_block, ALU.add))
                after_act(2)
                step(dve.tensor_scalar(r["w"], r["u"], 1.0, None, ALU.add))
                step(dve.tensor_scalar(r["d"], r["w"], -1.0, None, ALU.add))
                step(dve.tensor_scalar(r["i"], r["d"], 0.0, None, ALU.is_equal))
                step(dve.tensor_tensor(r["d"], r["d"], r["i"], ALU.add))
                step(dve.reciprocal(r["rd"], r["d"]))
                after_act(3)
                step(dve.tensor_tensor(r["lw"], r["lw"], r["i"], ALU.add))
                step(dve.tensor_tensor(r["v"], r["u"], r["lw"], ALU.mult))
                step(dve.tensor_tensor(r["v"], r["v"], r["rd"], ALU.mult))
                step(dve.scalar_tensor_tensor(r["sp"], r["z"], 0.0, r["v"], ALU.max, ALU.add))
                step(dve.tensor_scalar(r["sp"], r["sp"], 2.0 ** -LN_FLOOR, None, ALU.max))
                step(dve.tensor_scalar(r["mn"], r["z"], LN_FLOOR * float(np.log(2.0)), 0.0, ALU.add, ALU.min))
                after_act(4)
                step(dve.tensor_tensor(r["L"], r["L"], r["mn"], ALU.add))
                after_act(5)
                step(dve.tensor_tensor(r["b"], r["s"], gb[:, :], ALU.add))
                b = R["b"][:, :].rearrange("p (b e) -> p b e", b=TB)
                other = b.unsqueeze(2).to_broadcast([P, TB, E, E])
                own = b.unsqueeze(3).to_broadcast([P, TB, E, E])
                gt4, eq4 = (t[:, :, :].rearrange("p (b e) f -> p b e f", b=TB) for t in (gt, eq))
                dve.wait_ge(s_eof, 2)
                step(dve.tensor_tensor(gt4, other, own, ALU.is_gt), wait=False)
                step(dve.tensor_tensor(eq4, other, own, ALU.is_equal))
                first = lower[:, :, :].rearrange("p e f -> p (e f)").unsqueeze(1).to_broadcast([P, TB, E * E])
                eq3 = eq[:, :, :].rearrange("p (b e) f -> p b (e f)", b=TB)
                step(dve.tensor_tensor(eq3, eq3, first, ALU.mult))
                step(dve.tensor_tensor(gt[:, :, :], gt[:, :, :], eq[:, :, :], ALU.add))
                step(dve.tensor_reduce(r["rank"], gt[:, :, :], AX_X, ALU.add))
                step(dve.scalar_tensor_tensor(r["cw"], r["rank"], 2.0, r["s"], ALU.is_lt, ALU.mult))
                dve.wait_ge(s_cwone, f + 1)
                cw = R["cw"][:, :].rearrange("p (b e) -> p b e", b=TB)
                dve.tensor_copy(cw_rows[:, :, 0:E], cw)
                step(dve.tensor_copy(cw_rows[:, :, 32:32 + E], cw), wait=False)
                assert steps[0] == RT_DVE * (f + 1)
                dve.wait_ge(s_cwhi, f + 1)
                low = cwT[32:64, :]
                dve.tensor_tensor(low, ps[32:64, G_BANK:G_BANK + 2, :].rearrange("p a t -> p (a t)"),
                                  low.bitcast(F32), ALU.subtract).then_inc(s_cwT, 1)

                def lo(g):
                    dve.wait_ge(s_hhi, g + 1)
                    dve.tensor_tensor(hT_lo[:, g % HRING, :], ff_h[:, g % 2, :],
                                      hT_hi[:, g % HRING, :].bitcast(F32), ALU.subtract).then_inc(s_hlo, 1)

                def add_half(half):
                    dve.wait_ge(s_down, 2 * JT * f + JT * (half + 1))
                    for k in range(2):
                        rows = x[:, half * HB + 2 * k:half * HB + 2 * k + 2, :].rearrange("p b c -> p (b c)")
                        dve.scalar_tensor_tensor(rows, ps[:, ACC_BANK + k, :], 0.5, rows, ALU.mult, ALU.add)\
                            .then_inc(s_acc, 1)

                for u in range(2 * JT):
                    g = 2 * JT * f + u
                    dve.wait_ge(s_silu, g + 1)
                    dve.wait_ge(s_b, g + 1)
                    need(dve, s_h, g - 1)
                    dve.tensor_tensor(ff_m[:, g % 2, :], ps[:, B_BANK + g % 2, :], ff_s[:, g % 2, :], ALU.mult)\
                        .then_inc(s_m, 1)
                    dve.wait_ge(s_m, g + 1)
                    dve.wait_ge(s_g, g + 1)
                    need(dve, s_hlo, g - 1)
                    dve.tensor_tensor(ff_h[:, g % 2, :], ps[:, G_BANK + g % 2, :], ff_m[:, g % 2, :], ALU.mult)\
                        .then_inc(s_h, 1)
                    if u:
                        lo(g - 1)
                    if u == JT + 1:
                        add_half(0)
                lo(2 * JT * (f + 1) - 1)
                add_half(1)

            layer_norm(0)
            dve.wait_ge(s_in_b, 16)
            dve.tensor_copy(up_b[:, :, 0:J], stage_b).then_inc(s_cast_b, 1)
            ffn(0)
            dve.wait_ge(s_acc, 4)
            layer_norm(1)

            def bias_and_min(i, par, t):
                dve.wait_ge(s_scored, TB * i + t + 1)
                if t == 0:
                    dve.wait_ge(s_alibi, i + 1)
                u = t - 3
                need(dve, s_pt, NCH * i + FIRST[u] + len(CHUNKS[u]) if u >= 0
                     else NCH * (i - 1) + FIRST[TB + u] + len(CHUNKS[TB + u]))
                dve.memset(carrier[:, :], 0.0)
                k = P * (t + 1)
                dve.tensor_tensor_reduce(out=srow[:, P * ROW_AT[t]:P * ROW_AT[t] + k], in0=scores[:, 0:k], in1=alibi[:, par, T - k:T],
                                         scale=1.0, scalar=3e38, op0=ALU.add, op1=ALU.min,
                                         accum_out=neg_max[:, par, t:t + 1]).then_inc(s_ttr, 1)

            def pt_lo(i, t):
                for c, (b0, nb) in enumerate(CHUNKS[t]):
                    ch = NCH * i + FIRST[t] + c
                    dve.wait_ge(s_pthi, ch + 1)
                    dve.tensor_tensor(pair_part(pT_lo, t, b0, nb), chunk_bank(t, c, nb),
                                      pair_part(pT_hi, t, b0, nb).bitcast(F32), ALU.subtract).then_inc(s_ptlo, 1)

            def x_lo(use, half, dst, hi, scale):
                dve.wait_ge(s_xhi, use + 1)
                dve.scalar_tensor_tensor(dst, ps[:, X_BANK[half], :], scale[:, :], hi.bitcast(F32), ALU.mult, ALU.subtract)\
                    .then_inc(s_xlo, 1)

            def half_of(tile, par, half):
                return tile[:, par, half * HT:(half + 1) * HT]

            def qk_sum(n, half):
                dve.wait_ge(s_sq, 2 * n + half + 1)
                dve.tensor_reduce(qk_ss[:, half, :], sq[:, :, :].rearrange("p b (a d) -> p (b a) d", a=2), AX_X,
                                  ALU.add).then_inc(s_qkss, 1)

            def y_lo(h, half):
                dve.wait_ge(s_yhi, 2 * h + half + 1)
                dve.wait_ge(s_ysq, 2 * h + half + 1)
                dst = (slice(None), half_columns(half))
                dve.scalar_tensor_tensor(yT_lo[dst], ps[:, Y_BANK[half], :], y_scale[:, :], yT_hi[dst].bitcast(F32),
                                         ALU.mult, ALU.subtract).then_inc(s_ylo, 1)

            def y_norm(h, par):
                sums = row_sum[:, par, :]
                dve.scalar_tensor_tensor(y_e[:, :], sums, EPS, sums, ALU.mult, ALU.mult).then_inc(s_ye, 1)
                dve.wait_ge(s_yss, h + 1)
                dve.wait_ge(s_ye, h + 1)
                dve.scalar_tensor_tensor(y_t[:, :], y_sums, 1.0 / D, y_e[:, :],
                                         ALU.mult, ALU.add).then_inc(s_yt, 1)

            def add_projection(h, u):
                dve.wait_ge(s_pj, 4 * h + u + 1)
                if u == 0:
                    dve.wait_ge(s_yf, h + 1)
                for k in range(2):
                    rows = x[:, 2 * u + k, :]
                    last = dve.scalar_tensor_tensor(rows, ps[:, M_BANK + u % 2, k * C:(k + 1) * C],
                                                    y_f[:, 2 * u + k:2 * u + k + 1], rows, ALU.mult, ALU.add)
                last.then_inc(s_pjadd, 1)

            def body(i, it, par):
                att, nxt, prev, after = parts(i)
                n = i + 1
                for t in range(TB):
                    if nxt and t == 7:
                        bias_and_min(n, 1 - par, 1)
                    if att:
                        pt_lo(i, t)
                    if att and t < TB - 2:
                        bias_and_min(i, par, t + 2)
                    if att and t < 2:
                        lo, hi, pos, scale = ((kT_lo, kT_hi, KB, k_scale), (qT_lo, qT_hi, QB, q_scale))[t]
                        x_lo(xuse(i, pos), 1, half_of(lo, par, 1), half_of(hi, par, 1), scale)
                    if nxt and t in (4, 5):
                        lo, hi, pos, scale = ((kT_lo, kT_hi, KA, k_scale), (qT_lo, qT_hi, QA, q_scale))[t - 4]
                        x_lo(xuse(i, pos), 0, half_of(lo, 1 - par, 0), half_of(hi, 1 - par, 0), scale)
                    if nxt and t == 2:
                        qk_sum(n, 0)
                    if prev and t == 2:
                        y_lo(i - 1, 1)
                    if prev and t == 3:
                        y_norm(i - 1, 1 - par)
                    if nxt and t == 5:
                        qk_sum(n, 1)
                    if nxt and t == 6:
                        bias_and_min(n, 1 - par, 0)
                    if att and t == 7:
                        y_lo(i, 0)
                    if prev and t >= HB:
                        add_projection(i - 1, t - HB)

            run_heads(dve, body)
            dve.wait_ge(s_pjadd, 4 * H)
            layer_norm(2)
            ffn(1)

        @block.tensor
        def _(pe):
            pe.wait_ge(s_const, 3)

            def layer_norm(k):
                for half in range(2):
                    pe.wait_ge(s_xn, TB * k + HB * (half + 1))
                    for c in range(CC):
                        for b in range(HB):
                            last = pe.transpose(ps[:, 2 * half + c, b * P:(b + 1) * P],
                                                xn[:, half * HB + b, c * P:(c + 1) * P], ident[:, :])
                        last.then_inc(s_xtr, 1)

            def ffn(f):
                pe.wait_ge(s_xTlo, 4 * (f * 2 + 1))
                pe.wait_ge(s_gw, 2)
                for tb in range(TB):
                    for n, (c, part) in enumerate((c, part) for c in range(CC) for part in (xT_hi, xT_lo)):
                        last = pe.matmul(ps[:, G_BANK, tb * 2 * E:(tb + 1) * 2 * E], part[:, c, tb * P:(tb + 1) * P],
                                         gw2[:, c, :], start=n == 0, stop=n == 3)
                last.then_inc(s_logit, 1)

                def product(bank, weights, jt, half):
                    for n, (c, part) in enumerate((c, part) for c in range(CC) for part in (xT_hi, xT_lo)):
                        last = pe.matmul(ps[:, bank, :], weights[:, c, jt * P:(jt + 1) * P],
                                         part[:, c, half * HT:(half + 1) * HT], start=n == 0, stop=n == 3)
                    return last

                def combine_rows():
                    pe.wait_ge(s_rt_dve, RT_DVE * (f + 1))
                    for tb in range(TB):
                        last = pe.transpose(ps[:, G_BANK + tb // HB, (tb % HB) * P:(tb % HB + 1) * P],
                                            cw_rows[:, tb, :], ident[:, :])
                    last.then_inc(s_cwtr, 1)
                    pe.wait_ge(s_expert, 16)
                    pe.wait_ge(s_cwT, f + 1)

                def up(g, half, jt):
                    if g == 0:
                        pe.wait_ge(s_cast_a, 1)
                        pe.wait_ge(s_cast_b, 1)
                    need(pe, s_silu, g - 1)
                    product(A_BANK + g % 2, up_a, jt, half).then_inc(s_a, 1)
                    need(pe, s_m, g - 1)
                    product(B_BANK + g % 2, up_b, jt, half).then_inc(s_b, 1)

                def spread(g, half, jt):
                    need(pe, s_h, g - 1)
                    pe.matmul(ps[:, G_BANK + g % 2, :], expert_of[:, jt * P:(jt + 1) * P],
                              cwT[:, half * HT:(half + 1) * HT], start=True, stop=True).then_inc(s_g, 1)

                def back(g, half, jt):
                    if jt == 0 and half == 0:
                        pe.wait_ge(s_cast_d, f + 1)
                    if jt == 0:
                        need(pe, s_acc, 2 * (2 * f + half))
                    pe.wait_ge(s_hlo, g + 1)
                    for b in range(HB):
                        for part in (hT_hi, hT_lo):
                            last = pe.matmul(ps[:, ACC_BANK + b // 2, (b % 2) * C:(b % 2 + 1) * C],
                                             part[:, g % HRING, b * P:(b + 1) * P], down[:, jt, :],
                                             start=jt == 0 and part is hT_hi and b % 2 == 0,
                                             stop=jt == JT - 1 and part is hT_lo, skip_group_check=True)
                    last.then_inc(s_down, 1)

                units = [(2 * JT * f + JT * half + jt, half, jt) for half in range(2) for jt in range(JT)]
                for n, unit in enumerate(units):
                    up(*unit)
                    if n == 1:
                        combine_rows()
                        spread(*units[0])
                    if n:
                        spread(*unit)
                    if n >= 2:
                        back(*units[n - 2])
                back(*units[-2])
                back(*units[-1])

            layer_norm(0)
            ffn(0)
            layer_norm(1)
            pe.wait_ge(s_xTlo, 8)

            def score(i, par, t):
                if t == 0:
                    pe.wait_ge(s_xlo, xuse(i - 1, QA) + 1)
                if t == HB:
                    pe.wait_ge(s_xlo, xuse(i, QB) + 1)
                need(pe, s_ttr, TB * i + t)
                q = slice(t * P, (t + 1) * P)
                for c0 in range(0, t + 1, 4):
                    k = slice(c0 * P, min(t + 1, c0 + 4) * P)
                    for n, (a, b) in enumerate(((qT_hi, kT_hi), (qT_hi, kT_lo), (qT_lo, kT_hi))):
                        last = pe.matmul(scores[:, k], a[:, par, q], b[:, par, k], start=n == 0, stop=n == 2)
                last.then_inc(s_scored, 1)

            def project_qkv(n, tb):
                if tb == 0:
                    pe.wait_ge(s_wlo, n + 1)
                if tb < 2:
                    need(pe, s_pjadd, 4 * (n - 2) - 1 + tb)
                else:
                    need(pe, s_row, TB * n + tb - 1)
                last_of = 3 * CC - 1
                m = 0
                for c in range(CC):
                    for a, b in ((xT_hi, w_hi), (xT_hi, w_lo), (xT_lo, w_hi)):
                        last = pe.matmul(ps[:, M_BANK + tb % 2, 0:3 * D], a[:, c, tb * P:(tb + 1) * P], b[:, c, :],
                                         start=m == 0, stop=m == last_of)
                        m += 1
                last.then_inc(s_qkv, 1)

            def transpose_p(i, t):
                pe.wait_ge(s_exp, TB * i + t + 1)
                for c, (b0, nb) in enumerate(CHUNKS[t]):
                    need(pe, s_ptlo, NCH * i + FIRST[t] + c - 1)
                    for b in range(nb):
                        last = pe.transpose(ps[:, PT_BANK + (FIRST[t] + c) % 2, b * P:(b + 1) * P],
                                            srow[:, (ROW_AT[t] + b0 + b) * P:(ROW_AT[t] + b0 + b + 1) * P],
                                            ident[:, :])
                    last.then_inc(s_pt, 1)

            def values(i, par, u, part, has_next=True):
                if part == 0:
                    if u == 0:
                        pe.wait_ge(s_vlo, i + 1)
                        pe.wait_ge(s_xlo, xuse(i, QB) + 1)
                    if u == 2:
                        pe.wait_ge(s_xlo, xuse(i, QA) + 1 if has_next else xuse(i, QB) + 1)
                        need(pe, s_yt, i)
                    t = 2 * u + 1
                    pe.wait_ge(s_ptlo, NCH * i + FIRST[t] + len(CHUNKS[t]))
                blocks = 2 * u + 2
                for s in range(part * (u + 1), (part + 1) * (u + 1)):
                    first = P if s == blocks - 1 else 0
                    out_ = ps[:, Y_BANK[u // 2], (u % 2) * 2 * P + first:(u % 2 + 1) * 2 * P]
                    for m, (a, b) in enumerate(((v_hi, pT_hi), (v_hi, pT_lo), (v_lo, pT_hi))):
                        last = pe.matmul(out_, a[:, par, s, :], b[:, PAIR_AT[u] + s, first:],
                                         start=s == 0 and m == 0, stop=s == blocks - 1 and m == 2,
                                         skip_group_check=True)
                if u % 2 and part:
                    last.then_inc(s_pv, 1)

            def sum_squares(h):
                pe.wait_ge(s_ylo, 2 * (h + 1))
                for b in range(TB):
                    last = pe.matmul(y_sums[:, b:b + 1], ysq[:, b * P:(b + 1) * P], ones[:, :],
                                     start=True, stop=True)
                last.then_inc(s_yss, 1)

            def transpose_half(use, half, ready, count, blocks):
                pe.wait_ge(ready, count)
                need(pe, s_xlo, use)
                for b, block_ in enumerate(blocks):
                    last = pe.transpose(ps[:, X_BANK[half], b * P:(b + 1) * P], block_, ident[:, :])
                last.then_inc(s_xt, 1)

            def qk_blocks(half, which):
                return [qkv[:, half * HB + b, which * D:(which + 1) * D] for b in range(HB)]

            def project_y(h, q, rows):
                if q == 0:
                    pe.wait_ge(s_wplo, h + 1)
                if q < 2:
                    need(pe, s_row, rows + q)
                else:
                    need(pe, s_pjadd, 4 * h + q - 1)
                for k in range(2):
                    b = 2 * q + k
                    for m, (a, w) in enumerate(((yT_hi, wp_hi), (yT_hi, wp_lo), (yT_lo, wp_hi))):
                        last = pe.matmul(ps[:, M_BANK + q % 2, k * C:(k + 1) * C], a[:, b * P:(b + 1) * P], w[:, :],
                                         start=m == 0, stop=m == 2)
                last.then_inc(s_pj, 1)

            def body(i, it, par):
                att, nxt, prev, after = parts(i)
                n = i + 1
                for t in range(TB):
                    if att:
                        transpose_p(i, t)
                    if att and t < TB - 2:
                        score(i, par, t + 2)
                    if nxt and t < HB:
                        project_qkv(n, 2 * t)
                    if att and t < 2:
                        if t == 0:
                            need(pe, s_ylo, 2 * (i - 1) + 1)
                        transpose_half(xuse(i, (KB, QB)[t]), 1, s_qkn, 2 * i + 2, qk_blocks(1, 1 - t))
                    if nxt and t in (4, 5):
                        if prev and t == 4:
                            pe.wait_ge(s_yt, i)
                        transpose_half(xuse(i, (KA, QA)[t - 4]), 0, s_qkn, 2 * n + 1, qk_blocks(0, 5 - t))
                    if nxt and t == 7:
                        score(n, 1 - par, 1)
                    if prev and t >= HB:
                        project_y(i - 1, t - HB, TB * n + 7 if nxt else TB * H - 1)
                    if nxt and t == 6:
                        score(n, 1 - par, 0)
                    if prev and t < 2:
                        values(i - 1, 1 - par, 3, t)
                    if att and t > 1:
                        values(i, par, (t - 2) // 2, t % 2, nxt)
                    if nxt and t < HB:
                        project_qkv(n, 2 * t + 1)
                    if prev and t == 3:
                        sum_squares(i - 1)

            run_heads(pe, body)
            layer_norm(2)
            ffn(1)


def kernel(**inputs):
    import concourse.bacc as bacc
    from concourse.bass_utils import run_bass_kernel_spmd

    g = {k.removeprefix("L0_"): np.asarray(v) for k, v in inputs.items()}
    x = g["attn_x"]
    _, T, C = x.shape
    H, D = 16, P
    E = g["ffn_gate_w"].shape[0]

    def heads(w):
        return w.reshape(C // P, P, H, D).transpose(2, 1, 0, 3)

    def columns(w, shared):
        return np.concatenate([w.reshape(-1, C), shared], axis=0).T

    arrays = {
        "x_in": x.reshape(T, C),
        "w_qkv": np.concatenate([heads(g["attn_Wq"]), heads(g["attn_Wk"]), heads(g["attn_Wv"])], axis=3),
        "w_proj": g["attn_Wproj"].reshape(H, D, C),
        "q_w": g["attn_q_rms_w"].reshape(D, 1),
        "k_w": g["attn_k_rms_w"].reshape(D, 1),
        "y_w": g["attn_subln_w"].reshape(D, 1),
        "gate_w": g["ffn_gate_w"].T,
        "gate_b": np.tile(g["ffn_gate_b"], (P, T // P)),
        "w_up_a": columns(g["ffn_w1"], g["ffn_sw1"]),
        "w_up_b": columns(g["ffn_w3"], g["ffn_sw3"]),
        "w_down": np.concatenate([g["ffn_w2"].transpose(0, 2, 1).reshape(-1, C), g["ffn_sw2"].T], axis=0),
    }
    arrays = {k: np.ascontiguousarray(v) for k, v in arrays.items()}
    nc = bacc.Bacc("TRN2", target_bir_lowering=False, num_devices=1)
    aps = [nc.dram_tensor(k, v.shape, mybir.dt.from_np(v.dtype), kind="ExternalInput").ap() for k, v in arrays.items()]
    out = nc.dram_tensor("out", (T, C), F32, kind="ExternalOutput").ap()
    macaron_kernel(nc, *aps, out)
    result = run_bass_kernel_spmd(nc, [arrays], core_ids=[0])
    return result.results[0]["out"].reshape(x.shape)
```

```python
from contextlib import ExitStack

import numpy as np

import concourse.bass as bass
from concourse import mybir

F32 = mybir.dt.float32
F32R = mybir.dt.float32r
BF16 = mybir.dt.bfloat16
ALU = mybir.AluOpType
ACT = mybir.ActivationFunctionType
AX_X = mybir.AxisListType.X

P = 128
EPS = 1e-5
MASKED = 1e30
LN_FLOOR = 60
BANK = 512


def need(engine, semaphore, count):
    if not isinstance(count, int) or count > 0:
        engine.wait_ge(semaphore, count)


def macaron_kernel(nc, x_in, w_qkv, w_proj, q_w, k_w, y_w, gate_w, gate_b, w_up_a, w_up_b, w_down, out):
    T, C = x_in.shape
    H = w_qkv.shape[0]
    D = P
    E = gate_w.shape[1]
    J = w_down.shape[0]
    INTER = J // (E + 1)
    TB = T // P
    CC = C // P
    JT = -(-J // P)
    JPAD = JT * P
    JTAIL = J - (JT - 1) * P
    JR = INTER * E
    SHARED = JT - JR // P
    HB = TB // 2
    HT = T // 2
    assert (T, C, D) == (1024, 256, 128) and HT == BANK and JR % P == 0

    SLOPE = [2.0 ** (-8.0 / H * (h + 1)) for h in range(2)]
    SLOPE_STEP = 2.0 ** (-8.0 / H * 2)
    QSCALE = -float(D) ** -0.5

    CHUNKS = [[(c, min(4, t + 1 - c)) for c in range(0, t + 1, 4)] for t in range(TB)]
    FIRST = [sum(len(CHUNKS[u]) for u in range(t)) for t in range(TB)]
    NCH = sum(len(c) for c in CHUNKS)

    with ExitStack() as ctx:
        def sb(name, shape, dt=F32):
            return ctx.enter_context(nc.sbuf_tensor(name, shape, dt))

        def sem(name):
            return ctx.enter_context(nc.semaphore(name))

        x = sb("x", [P, TB, C])
        xT_hi = sb("xT_hi", [P, CC, T], F32R)
        xT_lo = sb("xT_lo", [P, CC, T], F32R)
        ident = sb("ident", [P, P])
        ROW_AT = [18, 12, 15, 8, 0, 15, 8, 0]
        srow = sb("srow", [P, 21 * P])
        stage_a = srow[:, HB * C:].bitcast(BF16)[:, 0:CC * J].rearrange("p (c j) -> p c j", c=CC)
        PAIR_AT = [8, 0, 8, 0]
        pT_hi = sb("pT_hi", [P, 14, 2 * P], F32R)
        pT_lo = sb("pT_lo", [P, 14, 2 * P], F32R)
        qkv = sb("qkv", [P, TB, 3 * D])
        sq = sb("sq", [P, HB, 2 * D])
        qT_hi = sb("qT_hi", [P, 2, T], F32R)
        qT_lo = sb("qT_lo", [P, 2, T], F32R)
        kT = sb("kT", [P, 2, 2, T], F32R)
        kT_hi, kT_lo = kT[:, 0, :, :], kT[:, 1, :, :]
        v_hi = sb("v_hi", [P, 2, TB, D], F32R)
        v_lo = sb("v_lo", [P, 2, TB, D], F32R)
        raw = sb("raw", [P, 2 * (CC * 3 * D + C)])
        wraw = raw[:, 0:2 * CC * 3 * D].rearrange("p (a c d) -> p a c d", a=2, c=CC)
        wpraw = raw[:, 2 * CC * 3 * D:].rearrange("p (a c) -> p a c", a=2)
        stage_d = raw[:, :].bitcast(BF16)[:, 0:JT * C].rearrange("p (t c) -> p t c", t=JT)
        w_hi = sb("w_hi", [P, CC, 3 * D], F32R)
        w_lo = sb("w_lo", [P, CC, 3 * D], F32R)
        wp_hi = sb("wp_hi", [P, C], F32R)
        wp_lo = sb("wp_lo", [P, C], F32R)
        alibi = sb("alibi", [P, 2, T])
        stage_b = alibi[:, :, :].rearrange("p a t -> p (a t)").bitcast(BF16)[:, 0:CC * J].rearrange(
            "p (c j) -> p c j", c=CC)
        yT_hi = sb("yT_hi", [P, T], F32R)
        yT_lo = sb("yT_lo", [P, T], F32R)
        ysq = sb("ysq", [P, T])
        up_a = sb("up_a", [P, CC, JPAD], F32R)
        up_b = sb("up_b", [P, CC, JPAD], F32R)
        down = kT[:, :, :, :].rearrange("p a b t -> p (a b t)")[:, 0:JT * C].rearrange("p (t c) -> p t c", t=JT)
        expert_of = sb("expert_of", [P, JR], F32R)
        xn = [t[:, 0:HB * C].rearrange("p (b c) -> p b c", c=C) for t in (ysq, srow)]
        cwT = qT_hi[:, 0, :]
        gt, eq = (ysq[:, k * TB * E * E:(k + 1) * TB * E * E].rearrange("p (b f) -> p b f", f=E) for k in range(2))
        flat = qkv[:, :, :].rearrange("p b d -> p (b d)")
        LAG = 4
        SRING = LAG + 1
        ff_s = flat[:, 0:SRING * BANK].rearrange("p (r t) -> p r t", r=SRING)
        ff_m = srow[:, 0:SRING * BANK].rearrange("p (r t) -> p r t", r=SRING)
        ff_h = sq[:, :, :].rearrange("p b d -> p (b d)").rearrange("p (r t) -> p r t", r=2)
        HRING = 3
        hT_hi, hT_lo = (t[:, 0:2 * HRING, :].rearrange("p a t -> p (a t)").rearrange("p (r t) -> p r t", t=BANK)
                        for t in (pT_hi, pT_lo))
        cw_rows = sq[:, :, :].rearrange("p a (r e) -> p (a r) e", e=P)
        expert_f = flat[:, 0:T]
        lgT = flat[0:2 * E, T:2 * T]

        bn = sb("bn", [P, TB, 6])
        mv = sb("mv", [P, TB, 2])
        neg_mean = sb("neg_mean", [P, TB])
        shift = sb("shift", [P, TB])
        lnv = sb("lnv", [P, TB])
        rstd = sb("rstd", [P, TB])
        qk_ss = sb("qk_ss", [P, 2, HB * 2])
        qk_ln = sb("qk_ln", [P, 2, HB * 2])
        qk_r = sb("qk_r", [P, 2, HB * 2])
        y_e = sb("y_e", [P, TB])
        y_t = sb("y_t", [P, TB])
        y_ln = sb("y_ln", [P, TB])
        y_f = sb("y_f", [P, TB])
        ones = sb("ones", [P, 1])
        neg_max = sb("neg_max", [P, 2, TB])
        row_sum = sb("row_sum", [P, 2, TB])
        q_w_sb = sb("q_w_sb", [P, 1])
        q_scale = sb("q_scale", [P, 1])
        k_scale = sb("k_scale", [P, 1])
        y_scale = sb("y_scale", [P, 1])
        epst = sb("epst", [P, 1])
        slope_step = sb("slope_step", [P, 1])
        carrier = sb("carrier", [P, 1])
        gw = sb("gw", [P, CC, E])
        gw2 = sb("gw2", [P, CC, P], F32R)
        gb = sb("gb", [P, TB * E])
        lower = sb("lower", [P, E, E])
        R = {n: sb("r_" + n, [P, TB * E]) for n in
             ("z", "a", "u", "w", "lw", "d", "i", "rd", "v", "sp", "L", "mn", "s", "b")}
        R |= {"rank": R["d"], "cw": R["w"]}

        ps = ctx.enter_context(nc.psum_tensor("ps", [P, 8, BANK], F32))
        PT_BANK, M_BANK = 2, 4
        Y_BANK = (7, 6)
        X_BANK = (6, 7)
        A_BANKS, B_BANKS, G_BANK, ACC_BANK = (0, 1, 6), (2, 3, 7), 4, 6
        scores = ps[:, 0:2, :].rearrange("p a t -> p (a t)")

        def y_sums(last_head, half):
            return ps[:, half if last_head else X_BANK[0], half * HB:(half + 1) * HB]



        s_x = [sem(f"s_x{i}") for i in range(2)]
        s_small = sem("s_small")
        s_in_a, s_in_b, s_in_d = sem("s_in_a"), sem("s_in_b"), sem("s_in_d")
        s_w = [sem(f"s_w{i}") for i in range(2)]
        s_wp = [sem(f"s_wp{i}") for i in range(2)]
        s_expert = sem("s_expert")
        s_out = sem("s_out")
        s_cast_b0 = sem("s_cast_b0")
        s_zeroed, s_const = sem("s_zeroed"), sem("s_const")
        s_cwzero = sem("s_cwzero")
        s_escratch, s_eof, s_dist, s_cast_d = sem("s_escratch"), sem("s_eof"), sem("s_dist"), sem("s_cast_d")
        s_alibi = sem("s_alibi")
        s_sq, s_qkn = sem("s_sq"), sem("s_qkn")
        s_wlo, s_wplo, s_vlo = sem("s_wlo"), sem("s_wplo"), sem("s_vlo")
        s_cast_a, s_lg0 = sem("s_cast_a"), sem("s_lg0")
        s_lnv, s_rstd, s_xThi = sem("s_lnv"), sem("s_rstd"), sem("s_xThi")
        s_shift, s_xn0 = sem("s_shift"), sem("s_xn0")
        s_rt_act, s_cwhi = sem("s_rt_act"), sem("s_cwhi")
        s_silu, s_hhi = sem("s_silu"), sem("s_hhi")
        s_exp, s_pthi, s_row = sem("s_exp"), sem("s_pthi"), sem("s_row")
        s_qkln, s_qkr, s_xhi, s_vhi = sem("s_qkln"), sem("s_qkr"), sem("s_xhi"), sem("s_vhi")
        s_yhi, s_ysq, s_yln, s_yf = sem("s_yhi"), sem("s_ysq"), sem("s_yln"), sem("s_yf")
        s_whi, s_wphi = sem("s_whi"), sem("s_wphi")
        s_gw, s_qs, s_lg1, s_cast_b1 = sem("s_gw"), sem("s_qs"), sem("s_lg1"), sem("s_cast_b1")
        s_bn, s_mv, s_xn, s_xTlo = sem("s_bn"), sem("s_mv"), sem("s_xn"), sem("s_xTlo")
        s_nm = sem("s_nm")
        s_rt_dve, s_cwT = sem("s_rt_dve"), sem("s_cwT")
        s_m, s_h, s_hlo, s_acc = sem("s_m"), sem("s_h"), sem("s_hlo"), sem("s_acc")
        s_ttr, s_ptlo, s_qkss, s_xlo = sem("s_ttr"), sem("s_ptlo"), sem("s_qkss"), sem("s_xlo")
        s_ylo, s_ye, s_yt, s_pjadd = sem("s_ylo"), sem("s_ye"), sem("s_yt"), sem("s_pjadd")
        s_lgT = sem("s_lgT")
        s_xtr, s_logit, s_cwtr = sem("s_xtr"), sem("s_logit"), sem("s_cwtr")
        s_a, s_b, s_g, s_down = sem("s_a"), sem("s_b"), sem("s_g"), sem("s_down")
        s_scored, s_pt, s_pv, s_qkv = sem("s_scored"), sem("s_pt"), sem("s_pv"), sem("s_qkv")
        s_xt, s_pj, s_yss = sem("s_xt"), sem("s_pj"), sem("s_yss")

        RT_DVE, RT_ACT = 22, 5

        block = ctx.enter_context(nc.Block())

        KB, QB, KA, QA = range(4)

        def xuse(i, pos):
            return 2 + 4 * i + pos

        def pair_part(pT, t, b0, nb):
            at = PAIR_AT[t // 2] + b0
            return pT[:, at:at + nb, (t % 2) * P:(t % 2 + 1) * P]

        def chunk_bank(t, c, nb):
            return ps[:, PT_BANK + (FIRST[t] + c) % 2, 0:nb * P].rearrange("p (b k) -> p b k", k=P)

        TILES = [[*range(JT - SHARED, JT), *range(JT - SHARED)], [*range(JT)]]
        WEIGHTED = 2 * (JT - SHARED)

        def weighted(d):
            return SHARED <= d < SHARED + WEIGHTED

        def weighted_before(f, d):
            return WEIGHTED * f + min(max(0, d - SHARED), WEIGHTED)

        def ab_slot(u):
            return u if u < 3 else (u + 1) % 2

        def ab_before(u):
            return u - 3 if u < 5 else u - 2

        def half_blocks(half):
            return slice(half * HB, (half + 1) * HB)

        def half_columns(half):
            return slice(half * HT, (half + 1) * HT)

        def run_heads(engine, body):
            for i in (-1, 0, 1):
                body(i, i // 2, i % 2)
            with engine.Fori(1, H // 2 - 1) as it:
                body(2 * it, it, 0)
                body(2 * it + 1, it, 1)
            for i in (H - 2, H - 1, H):
                body(i, i // 2, i % 2)

        def qk_steps(attention):
            return (HB, HB + 1) if attention else (HB - 1, HB)

        def projections_at(attention, t):
            if attention:
                return (t - HB,) if t >= HB else ()
            return {2: (0, 1), 4: (2,), 5: (3,)}.get(t, ())

        def qk_bank(attention, which):
            return 0 if attention else which

        def parts(i):
            if not isinstance(i, int):
                return True, True, True, True
            return 0 <= i < H, i + 1 < H, i >= 1, i + 2 < H

        @block.sync
        def _(sp):
            def load_down():
                sp.dma_start(stage_d[:, 0:JT - 1, :],
                             w_down[0:(JT - 1) * P, :].rearrange("(t p) c -> p t c", p=P)).then_inc(s_in_d, 16)

            def load_down_tail():
                sp.dma_start(stage_d[0:JTAIL, JT - 1, :], w_down[(JT - 1) * P:, :]).then_inc(s_in_d, 16)

            sp.dma_start(x[:, 0:HB, :], x_in[0:HT, :].rearrange("(b p) c -> p b c", p=P)).then_inc(s_x[0], 16)
            sp.dma_start(x[:, HB:, :], x_in[HT:, :].rearrange("(b p) c -> p b c", p=P)).then_inc(s_x[1], 16)
            for dst, src in ((gw[:, :, :], gate_w.rearrange("(c p) e -> p c e", p=P)), (gb[:, :], gate_b),
                             (q_w_sb[:, :], q_w), (k_scale[:, :], k_w), (y_scale[:, :], y_w)):
                sp.dma_start(dst, src).then_inc(s_small, 16)
            sp.dma_start(stage_a, w_up_a.rearrange("(c p) j -> p c j", p=P)).then_inc(s_in_a, 16)
            sp.dma_start(stage_b, w_up_b.rearrange("(c p) j -> p c j", p=P)).then_inc(s_in_b, 16)
            load_down()
            sp.wait_ge(s_zeroed, 3)
            load_down_tail()

            sp.wait_ge(s_eof, 2)
            sp.dma_start(expert_of[32:32 + E, :].bitcast(F32), expert_of[0:E, :].bitcast(F32)).then_inc(s_expert, 16)

            def load_w(n, slot):
                need(sp, s_wlo, n - 1)
                sp.dma_start(wraw[:, slot, :, :], w_qkv[n, :, :, :]).then_inc(s_w[slot], 16)

            def load_wp(n, slot):
                need(sp, s_wplo, n - 1)
                sp.dma_start(wpraw[:, slot, :], w_proj[n, :, :]).then_inc(s_wp[slot], 16)

            sp.wait_ge(s_cast_d, 1)
            for n in range(2):
                load_w(n, n)
                load_wp(n, n)
            for n in (2, 3):
                load_w(n, n % 2)
            with sp.Fori(2, H // 2) as it:
                for slot in range(2):
                    load_w(2 * it + slot, slot)
                    load_wp(2 * it + slot - 2, slot)
            for n in (H - 2, H - 1):
                load_wp(n, n % 2)
            sp.wait_ge(s_zeroed, 4)
            load_down()
            load_down_tail()
            for half in range(2):
                sp.wait_ge(s_acc, 2 * 3 + 2 * half)
                sp.dma_start(out[half * HT:(half + 1) * HT, :].rearrange("(b p) c -> p b c", p=P),
                             x[:, half * HB:(half + 1) * HB, :]).then_inc(s_out, 16)
            sp.wait_ge(s_out, 32)

        @block.gpsimd
        def _(pool):
            pool.memset(ident[:, :], 0.0).then_inc(s_zeroed, 1)
            pool.wait_ge(s_zeroed, 1)
            pool.affine_select(out=ident[:, :], in_=ident[:, :], compare_op=ALU.not_equal, fill=1.0, base=0,
                               pattern=[[-1, P]], channel_multiplier=1).then_inc(s_const, 1)
            pool.memset(epst[:, :], EPS).then_inc(s_const, 1)
            pool.memset(slope_step[:, :], SLOPE_STEP)
            pool.memset(ones[:, :], 1.0)
            pool.memset(lower[:, :, :], 1.0).then_inc(s_zeroed, 1)
            pool.wait_ge(s_zeroed, 2)
            pool.affine_select(out=lower[:, :, :], in_=lower[:, :, :], compare_op=ALU.is_gt, fill=0.0, base=0,
                               pattern=[[1, E], [-1, E]], channel_multiplier=0).then_inc(s_const, 1)
            pool.memset(up_a[:, :, J:JPAD].bitcast(F32), 0.0)
            pool.memset(up_b[:, :, J:JPAD].bitcast(F32), 0.0)
            pool.memset(stage_d[:, JT - 1, :], 0.0).then_inc(s_zeroed, 1)

            def clear_combine_rows(f):
                need(pool, s_qkss, 2 * H * f)
                pool.memset(cw_rows[:, :, :], 0.0).then_inc(s_cwzero, 1)

            clear_combine_rows(0)
            for n, lo in enumerate(range(0, JR, T)):
                k = min(T, JR - lo)
                need(pool, s_eof, n)
                pool.memset(expert_f[:, 0:k], 1.0).then_inc(s_escratch, 1)
                pool.wait_ge(s_escratch, 2 * n + 1)
                pool.affine_select(out=expert_f[:, 0:k], in_=expert_f[:, 0:k], compare_op=ALU.is_ge, fill=0.0,
                                   base=lo, pattern=[[1, k]], channel_multiplier=-INTER).then_inc(s_escratch, 1)
                pool.wait_ge(s_escratch, 2 * n + 2)
                pool.affine_select(out=expert_of[:, lo:lo + k], in_=expert_f[:, 0:k], compare_op=ALU.is_ge, fill=0.0,
                                   base=INTER - 1 - lo, pattern=[[-1, k]], channel_multiplier=INTER).then_inc(s_eof, 1)
            pool.wait_ge(s_in_b, 16)
            pool.tensor_copy(up_b[:, 0, 0:J], stage_b[:, 0, :]).then_inc(s_cast_b0, 1)
            pool.wait_ge(s_in_d, 32)
            pool.tensor_copy(down[:, :, :], stage_d[:, :, :]).then_inc(s_cast_d, 1)
            pool.wait_ge(s_cast_b0, 1)
            pool.wait_ge(s_cast_b1, 1)
            dist = alibi[:, 1, :]
            pool.iota(dist, pattern=[[-1, T]], base=T - P, channel_multiplier=1,
                      allow_small_or_imprecise_dtypes=True).then_inc(s_dist, 1)
            pool.wait_ge(s_dist, 1)
            pool.affine_select(out=dist, in_=dist, compare_op=ALU.is_ge, fill=MASKED, base=T - P,
                               pattern=[[-1, T]], channel_multiplier=1).then_inc(s_dist, 1)
            pool.wait_ge(s_dist, 2)
            pool.tensor_scalar(alibi[:, 0, :], dist, SLOPE[0], None, ALU.mult).then_inc(s_alibi, 1)
            pool.tensor_scalar(dist, dist, SLOPE[1], None, ALU.mult).then_inc(s_alibi, 1)

            def split_w(n, slot):
                pool.wait_ge(s_whi, n + 1)
                pool.tensor_tensor(w_lo[:, :, :], wraw[:, slot, :, :], w_hi[:, :, :].bitcast(F32), ALU.subtract)\
                    .then_inc(s_wlo, 1)

            def square_qk(n, half):
                pool.wait_ge(s_row, TB * n + HB * (half + 1))
                need(pool, s_qkss, 2 * n + half)
                qk = qkv[:, half * HB:(half + 1) * HB, 0:2 * D]
                pool.tensor_tensor(sq[:, :, :], qk, qk, ALU.mult).then_inc(s_sq, 1)

            def scale_qk(n, half):
                pool.wait_ge(s_qkr, 2 * n + half + 1)
                qk = qkv[:, half * HB:(half + 1) * HB, 0:2 * D].rearrange("p b (a d) -> p b a d", a=2)
                r = qk_r[:, half, :].rearrange("p (b a) -> p b a", a=2).unsqueeze(3).to_broadcast([P, HB, 2, D])
                pool.tensor_tensor(qk, qk, r, ALU.mult).then_inc(s_qkn, 1)

            split_w(0, 0)
            step_t = slope_step[:, :]

            def body(i, it, par):
                att, nxt, prev, after = parts(i)
                n = i + 1
                if prev and nxt:
                    pool.wait_ge(s_ttr, TB * i)
                    pool.tensor_tensor(alibi[:, 1 - par, :], alibi[:, 1 - par, :], step_t.to_broadcast([P, T]), ALU.mult)\
                        .then_inc(s_alibi, 1)
                if nxt:
                    square_qk(n, 0)
                if prev:
                    pool.wait_ge(s_wphi, i)
                    pool.tensor_tensor(wp_lo[:, :], wpraw[:, 1 - par, :], wp_hi[:, :].bitcast(F32), ALU.subtract)\
                        .then_inc(s_wplo, 1)
                if nxt:
                    scale_qk(n, 0)
                    square_qk(n, 1)
                    if not att:
                        split_w(i + 2, par)
                    pool.wait_ge(s_vhi, n + 1)
                    pool.tensor_tensor(v_lo[:, 1 - par, :, :], qkv[:, :, 2 * D:3 * D],
                                       v_hi[:, 1 - par, :, :].bitcast(F32), ALU.subtract).then_inc(s_vlo, 1)
                if after and att:
                    split_w(i + 2, par)
                if nxt:
                    scale_qk(n, 1)

            run_heads(pool, body)
            pool.wait_ge(s_wlo, H)
            pool.wait_ge(s_wplo, H)
            pool.memset(stage_d[:, JT - 1, :], 0.0).then_inc(s_zeroed, 1)
            clear_combine_rows(1)
            pool.wait_ge(s_scored, TB * H)
            pool.wait_ge(s_in_d, 64)
            pool.tensor_copy(down[:, :, :], stage_d[:, :, :]).then_inc(s_cast_d, 1)

        @block.scalar
        def _(act):
            def norm_factors(m):
                half = slice(m % 2 * HB, (m % 2 + 1) * HB)
                act.wait_ge(s_mv, m + 1)
                act.activation(lnv[:, half], mv[:, half, 1], ACT.Ln, bias=epst[:, :]).then_inc(s_lnv, 1)
                act.wait_ge(s_lnv, m + 1)
                act.activation(rstd[:, half], lnv[:, half], ACT.Exp, scale=-0.5).then_inc(s_rstd, 1)

            def row_shifts(m):
                act.wait_ge(s_rstd, m + 1)
                act.wait_ge(s_nm, m // 2 + 1)
                for b in range(HB):
                    last = act.activation(shift[:, b:b + 1], neg_mean[:, b:b + 1], ACT.Copy, scale=rstd[:, b:b + 1])
                last.then_inc(s_shift, 1)

            def normalise(m, blocks=range(HB)):
                act.wait_ge(s_shift, m // 2 + 1)
                for b in blocks:
                    last = act.activation(xn[0][:, b, :], x[:, b, :], ACT.Identity, bias=shift[:, b:b + 1],
                                          scale=rstd[:, b:b + 1])
                if HB - 1 in blocks:
                    last.then_inc(s_xn0, 1)

            def stream_hi(m):
                for c in range(CC):
                    act.wait_ge(s_xtr, CC * m + c + 1)
                    act.activation(xT_hi[:, c, half_columns(m % 2)], ps[:, 2 * (m % 2) + c, :], ACT.Copy)\
                        .then_inc(s_xThi, 1)

            def copy_logits(f):
                act.wait_ge(s_lgT, 2 * f + 1)
                act.activation(lgT[:, 0:HT], ps[0:2 * E, G_BANK, :], ACT.Copy).then_inc(s_lg0, 1)

            def ffn(f):
                base = RT_DVE * f
                if f == 1:
                    copy_logits(1)
                for n, (name, src, func, scale, after_dve) in enumerate((
                        ("a", "z", ACT.Abs, 1.0, 2), ("u", "a", ACT.Exp, -1.0, 2), ("lw", "w", ACT.Ln, 1.0, 3),
                        ("L", "sp", ACT.Ln, 1.0, 12), ("s", "L", ACT.Exp, 0.5, 14))):
                    act.wait_ge(s_rt_dve, base + after_dve)
                    if n == 1:
                        act.wait_ge(s_rt_act, RT_ACT * f + 1)
                    act.activation(R[name][:, :], R[src][:, :], func, scale=scale).then_inc(s_rt_act, 1)
                act.preload_act_table_set("silu_and_others")

                def hi(d):
                    g = 2 * JT * f + d
                    if weighted(d):
                        w = weighted_before(f, d)
                        act.wait_ge(s_h, w + 1)
                        h = ff_h[:, w % 2, :]
                    else:
                        act.wait_ge(s_m, g + 1)
                        h = ff_m[:, g % SRING, :]
                    need(act, s_down, g - HRING + 1)
                    act.activation(hT_hi[:, g % HRING, :], h, ACT.Copy).then_inc(s_hhi, 1)

                for step in range(2 * JT + LAG):
                    g = 2 * JT * f + step
                    if step < 2 * JT:
                        if g == 0:
                            act.wait_ge(s_eof, 2)
                        act.wait_ge(s_a, g + 1)
                        need(act, s_m, g - SRING + 1)
                        act.activation(ff_s[:, g % SRING, :], ps[:, A_BANKS[ab_slot(step)], :], ACT.Silu).then_inc(s_silu, 1)
                    d = step - LAG
                    if d >= 1 and weighted(d - 1):
                        hi(d - 1)
                    if d >= 0 and d < 2 * JT and not weighted(d):
                        hi(d)
                    if d == 0:
                        for half in range(2):
                            act.wait_ge(s_cwtr, 2 * f + half + 1)
                            act.activation(cwT[:, half_columns(half)], ps[:, G_BANK + half, :], ACT.Copy)\
                                .then_inc(s_cwhi, 1)
                    if f == 0 and step == JT:
                        split_w(0, 0, 0)
                    if f == 0 and step == 2 * JT - 1:
                        act.preload_act_table_set("natural_log_exp_and_others")
                        norm_factors(2)
                        row_shifts(2)
                    if f == 0 and step in (2 * JT, 2 * JT + 1):
                        k = 2 * (step - 2 * JT)
                        normalise(2, (k, k + 1))
                    if f == 0 and step == 2 * JT + 3:
                        stream_hi(2)

            def split_w(n, slot, use):
                act.wait_ge(s_w[slot], 16 * (use + 1))
                need(act, s_qkv, TB * n)
                act.activation(w_hi[:, :, :], wraw[:, slot, :, :], ACT.Copy).then_inc(s_whi, 1)

            act.preload_act_table_set("natural_log_exp_and_others")
            norm_factors(0)
            row_shifts(0)
            normalise(0)
            norm_factors(1)
            stream_hi(0)
            stream_hi(1)
            act.wait_ge(s_in_a, 16)
            act.activation(up_a[:, 0, 0:J], stage_a[:, 0, :], ACT.Copy).then_inc(s_cast_a, 1)
            copy_logits(0)
            act.activation(up_a[:, 1, 0:J], stage_a[:, 1, :], ACT.Copy).then_inc(s_cast_a, 1)
            ffn(0)

            def exp(i, par, t):
                act.wait_ge(s_ttr, TB * i + t + 1)
                row = srow[:, P * ROW_AT[t]:P * (ROW_AT[t] + t + 1)]
                act.activation(row, row, ACT.Exp, bias=neg_max[:, par, t:t + 1], scale=-1.0,
                               accum_out=row_sum[:, par, t:t + 1]).then_inc(s_exp, 1)

            def qkv_row(n, tb):
                act.wait_ge(s_qkv, TB * n + tb + 1)
                if tb == 0:
                    need(act, s_vlo, n)
                act.activation(qkv[:, tb, :], ps[:, M_BANK + tb % 2, 0:3 * D], ACT.Copy).then_inc(s_row, 1)

            def pt_hi(i, t):
                for c, (b0, nb) in enumerate(CHUNKS[t]):
                    ch = NCH * i + FIRST[t] + c
                    act.wait_ge(s_pt, ch + 1)
                    act.activation(pair_part(pT_hi, t, b0, nb), chunk_bank(t, c, nb), ACT.Copy).then_inc(s_pthi, 1)

            def x_hi(use, half, dst, scale):
                act.wait_ge(s_xt, use + 1)
                act.activation(dst, ps[:, X_BANK[half], :], ACT.Copy, scale=scale[:, :]).then_inc(s_xhi, 1)

            def half_of(tile, par, half):
                return tile[:, par, half * HT:(half + 1) * HT]

            def qk_rsqrt(n, half):
                act.wait_ge(s_qkss, 2 * n + half + 1)
                act.activation(qk_ln[:, half, :], qk_ss[:, half, :], ACT.Ln, scale=1.0 / D, bias=epst[:, :])\
                    .then_inc(s_qkln, 1)
                act.wait_ge(s_qkln, 2 * n + half + 1)
                act.activation(qk_r[:, half, :], qk_ln[:, half, :], ACT.Exp, scale=-0.5).then_inc(s_qkr, 1)

            def y_hi(h, half):
                act.wait_ge(s_pv, 2 * h + half + 1)
                need(act, s_pj, 4 * (h - 1) + 2 * half + 2)
                act.activation(yT_hi[:, half_columns(half)], ps[:, Y_BANK[half], :], ACT.Copy, scale=y_scale[:, :])\
                    .then_inc(s_yhi, 1)
                need(act, s_yss, h)
                act.activation(ysq[:, half_columns(half)], ps[:, Y_BANK[half], :], ACT.Square).then_inc(s_ysq, 1)

            def y_rsqrt(h, part, blocks):
                act.wait_ge(s_yt, h + part + 1)
                act.activation(y_ln[:, blocks], y_t[:, blocks], ACT.Ln).then_inc(s_yln, 1)
                act.wait_ge(s_yln, h + part + 1)
                act.activation(y_f[:, blocks], y_ln[:, blocks], ACT.Exp, scale=-0.5).then_inc(s_yf, 1)

            act.wait_ge(s_qs, 1)

            def body(i, it, par):
                att, nxt, prev, after = parts(i)
                n = i + 1
                for t in range(TB):
                    if not (att or prev) and t == 1:
                        norm_factors(3)
                    if not (att or prev) and t == 2:
                        stream_hi(3)
                        qk_rsqrt(n, 0)
                    if att:
                        pt_hi(i, t)
                    if nxt and t < HB:
                        qkv_row(n, 2 * t)
                    if att and t < 2:
                        dst, pos, scale = ((kT_hi, KB, k_scale), (qT_hi, QB, q_scale))[t]
                        x_hi(xuse(i, pos), 1, half_of(dst, par, 1), scale)
                    if nxt and t in qk_steps(att):
                        dst, pos, scale = ((kT_hi, KA, k_scale), (qT_hi, QA, q_scale))[qk_steps(att).index(t)]
                        x_hi(xuse(i, pos), qk_bank(att, pos - KA), half_of(dst, 1 - par, 0), scale)
                    if after and t == (5 if att else 4):
                        split_w(i + 2, par, it + 1)
                    if nxt and t == 4:
                        act.wait_ge(s_row, TB * (n + 1))
                        act.activation(v_hi[:, 1 - par, :, :], qkv[:, :, 2 * D:3 * D], ACT.Copy).then_inc(s_vhi, 1)
                    if att and t < TB - 3:
                        exp(i, par, t + 2)
                    if att and t == TB - 2:
                        exp(i, par, t + 1)
                    if nxt and t < HB:
                        qkv_row(n, 2 * t + 1)
                    if nxt and t == 7:
                        qk_rsqrt(n, 1)
                    if att and t == 7:
                        y_hi(i, 0)
                    if nxt and t >= TB - 2:
                        exp(n, 1 - par, t - (TB - 2))
                    if prev and t == 1:
                        wp_use = it - 1 + (par + 1) // 2
                        act.wait_ge(s_wp[1 - par], 16 * (wp_use + 1))
                        need(act, s_pj, 4 * (i - 1))
                        act.activation(wp_hi[:, :], wpraw[:, 1 - par, :], ACT.Copy).then_inc(s_wphi, 1)
                    if nxt and att and t == 2:
                        qk_rsqrt(n, 0)
                    if prev and t == 2:
                        y_hi(i - 1, 1)
                    if prev and att and t == 3:
                        y_rsqrt(i - 1, 0, slice(0, TB))
                    if prev and not att and t in (2, 3):
                        y_rsqrt(i - 1, t - 2, half_blocks(t - 2))

            run_heads(act, body)
            norm_factors(4)
            row_shifts(4)
            normalise(4)
            norm_factors(5)
            stream_hi(4)
            stream_hi(5)
            ffn(1)

        @block.vector
        def _(dve):
            def prepare_small():
                dve.wait_ge(s_small, 80)
                dve.tensor_copy(gw2[:, :, 0:E], gw[:, :, :]).then_inc(s_gw, 1)
                dve.tensor_scalar(q_scale[:, :], q_w_sb[:, :], QSCALE, None, ALU.mult).then_inc(s_qs, 1)
                dve.memset(gw2[:, :, 2 * E:P].bitcast(F32), 0.0)
                dve.wait_ge(s_gw, 1)
                dve.tensor_tensor(gw2[:, :, E:2 * E], gw[:, :, :], gw2[:, :, 0:E].bitcast(F32), ALU.subtract)\
                    .then_inc(s_gw, 1)

            def norm_stats(m):
                blocks = range(m % 2 * HB, (m % 2 + 1) * HB)
                if m < 2:
                    dve.wait_ge(s_x[m], 16)
                for tb in blocks:
                    last = dve.bn_stats(bn[:, tb, :], x[:, tb, :])
                last.then_inc(s_bn, 1)
                dve.wait_ge(s_bn, m + 1)
                for tb in blocks:
                    last = dve.bn_aggr(mv[:, tb, :], bn[:, tb, :])
                last.then_inc(s_mv, 1)
                if m % 2 == 0:
                    dve.wait_ge(s_mv, m + 1)
                    half = slice(0, HB)
                    dve.tensor_scalar(neg_mean[:, half], mv[:, half, 0], -1.0, None, ALU.mult).then_inc(s_nm, 1)

            def normalise(m):
                dve.wait_ge(s_rstd, m + 1)
                for b in range(HB):
                    tb = m % 2 * HB + b
                    last = dve.tensor_scalar(xn[m % 2][:, b, :], x[:, tb, :], mv[:, tb, 0:1], rstd[:, tb:tb + 1],
                                             ALU.subtract, ALU.mult)
                last.then_inc(s_xn, 1)

            def stream_lo(m):
                for c in range(CC):
                    dve.wait_ge(s_xThi, CC * m + c + 1)
                    dst = (slice(None), c, half_columns(m % 2))
                    dve.tensor_tensor(xT_lo[dst], ps[:, 2 * (m % 2) + c, :], xT_hi[dst].bitcast(F32), ALU.subtract)\
                        .then_inc(s_xTlo, 1)

            def ffn(f):
                def gate(u):
                    g = 2 * JT * f + u
                    dve.wait_ge(s_silu, g + 1)
                    dve.wait_ge(s_b, g + 1)
                    if u >= SRING:
                        before = u - SRING
                        if weighted(before):
                            dve.wait_ge(s_h, weighted_before(f, before) + 1)
                        else:
                            dve.wait_ge(s_hlo, g - SRING + 1)
                    dve.tensor_tensor(ff_m[:, g % SRING, :], ps[:, B_BANKS[ab_slot(u)], :], ff_s[:, g % SRING, :],
                                      ALU.mult).then_inc(s_m, 1)

                steps = [RT_DVE * f]

                def step(instruction, wait=True):
                    instruction.then_inc(s_rt_dve, 1)
                    steps[0] += 1
                    if wait:
                        dve.wait_ge(s_rt_dve, steps[0])

                def after_act(n):
                    dve.wait_ge(s_rt_act, RT_ACT * f + n)

                dve.wait_ge(s_lgT, 2 * f + 2)
                dve.tensor_copy(lgT[:, HT:T], ps[0:2 * E, G_BANK + 1, :]).then_inc(s_lg1, 1)

                r = {name: tile[:, :] for name, tile in R.items()}
                logits = ps[:, G_BANK, 0:TB * 2 * E].rearrange("p (b e) -> p b e", b=TB)
                by_block = R["v"][:, :].rearrange("p (b e) -> p b e", b=TB)
                dve.wait_ge(s_logit, f + 1)
                step(dve.tensor_copy(by_block, logits[:, :, E:2 * E]))
                step(dve.tensor_tensor(R["z"][:, :].rearrange("p (b e) -> p b e", b=TB), logits[:, :, 0:E],
                                       by_block, ALU.add))
                after_act(2)
                step(dve.tensor_scalar(r["w"], r["u"], 1.0, None, ALU.add))
                step(dve.tensor_scalar(r["d"], r["w"], -1.0, None, ALU.add))
                step(dve.tensor_scalar(r["i"], r["d"], 0.0, None, ALU.is_equal))
                step(dve.tensor_tensor(r["d"], r["d"], r["i"], ALU.add))
                step(dve.reciprocal(r["rd"], r["d"]))
                after_act(3)
                step(dve.tensor_tensor(r["lw"], r["lw"], r["i"], ALU.add))
                step(dve.tensor_tensor(r["v"], r["u"], r["lw"], ALU.mult))
                step(dve.tensor_tensor(r["v"], r["v"], r["rd"], ALU.mult))
                step(dve.scalar_tensor_tensor(r["sp"], r["z"], 0.0, r["v"], ALU.max, ALU.add))
                step(dve.tensor_scalar(r["sp"], r["sp"], 2.0 ** -LN_FLOOR, None, ALU.max))
                step(dve.tensor_scalar(r["mn"], r["z"], LN_FLOOR * float(np.log(2.0)), 0.0, ALU.add, ALU.min))
                after_act(4)
                step(dve.tensor_tensor(r["L"], r["L"], r["mn"], ALU.add))
                after_act(5)
                step(dve.tensor_tensor(r["b"], r["s"], gb[:, :], ALU.add))
                b = R["b"][:, :].rearrange("p (b e) -> p b e", b=TB)
                other = b.unsqueeze(2).to_broadcast([P, TB, E, E])
                own = b.unsqueeze(3).to_broadcast([P, TB, E, E])
                gt4, eq4 = (t[:, :, :].rearrange("p (b e) f -> p b e f", b=TB) for t in (gt, eq))
                step(dve.tensor_tensor(gt4, other, own, ALU.is_gt), wait=False)
                step(dve.tensor_tensor(eq4, other, own, ALU.is_equal))
                gate(0)
                first = lower[:, :, :].rearrange("p e f -> p (e f)").unsqueeze(1).to_broadcast([P, TB, E * E])
                eq3 = eq[:, :, :].rearrange("p (b e) f -> p b (e f)", b=TB)
                step(dve.tensor_tensor(eq3, eq3, first, ALU.mult))
                step(dve.tensor_tensor(gt[:, :, :], gt[:, :, :], eq[:, :, :], ALU.add))
                gate(1)
                step(dve.tensor_reduce(r["rank"], gt[:, :, :], AX_X, ALU.add))
                step(dve.scalar_tensor_tensor(r["cw"], r["rank"], 2.0, r["s"], ALU.is_lt, ALU.mult))
                dve.wait_ge(s_cwzero, f + 1)
                cw = R["cw"][:, :].rearrange("p (b e) -> p b e", b=TB)
                dve.tensor_copy(cw_rows[:, :, 0:E], cw)
                step(dve.tensor_copy(cw_rows[:, :, 32:32 + E], cw), wait=False)
                assert steps[0] == RT_DVE * (f + 1)
                gate(2)
                gate(3)

                def combine_lo():
                    for half in range(2):
                        dve.wait_ge(s_cwhi, 2 * f + half + 1)
                        low = cwT[32:64, half_columns(half)]
                        dve.tensor_tensor(low, ps[32:64, G_BANK + half, :], low.bitcast(F32), ALU.subtract)\
                            .then_inc(s_cwT, 1)

                def weigh(d):
                    g = 2 * JT * f + d
                    w = weighted_before(f, d)
                    dve.wait_ge(s_m, g + 1)
                    dve.wait_ge(s_g, w + 1)
                    need(dve, s_hlo, g - 1)
                    dve.tensor_tensor(ff_h[:, w % 2, :], ps[:, G_BANK + w % 2, :], ff_m[:, g % SRING, :], ALU.mult)\
                        .then_inc(s_h, 1)

                def lo(d):
                    g = 2 * JT * f + d
                    dve.wait_ge(s_hhi, g + 1)
                    h = ff_h[:, weighted_before(f, d) % 2, :] if weighted(d) else ff_m[:, g % SRING, :]
                    dve.tensor_tensor(hT_lo[:, g % HRING, :], h,
                                      hT_hi[:, g % HRING, :].bitcast(F32), ALU.subtract).then_inc(s_hlo, 1)

                def add_half(half):
                    dve.wait_ge(s_down, 2 * JT * f + JT * (half + 1))
                    for k in range(2):
                        rows = x[:, half * HB + 2 * k:half * HB + 2 * k + 2, :].rearrange("p b c -> p (b c)")
                        dve.scalar_tensor_tensor(rows, ps[:, ACC_BANK + k, :], 0.5, rows, ALU.mult, ALU.add)\
                            .then_inc(s_acc, 1)

                for step_ in range(LAG, 2 * JT + LAG):
                    d = step_ - LAG
                    if step_ < 2 * JT:
                        gate(step_)
                    if weighted(d):
                        weigh(d)
                    if d and weighted(d - 1):
                        lo(d - 1)
                    if not weighted(d):
                        lo(d)
                    if d == 0:
                        combine_lo()
                    if d == JT + 1:
                        add_half(0)
                    if f == 0 and d == JT + 3:
                        dve.wait_ge(s_acc, 2)
                        norm_stats(2)
                    if f == 0 and step_ == 2 * JT + 3:
                        stream_lo(2)
                add_half(1)

            dve.wait_ge(s_const, 3)
            for m in range(2):
                norm_stats(m)
            normalise(1)
            prepare_small()
            stream_lo(0)
            stream_lo(1)
            dve.wait_ge(s_in_b, 16)
            dve.tensor_copy(up_b[:, 1, 0:J], stage_b[:, 1, :]).then_inc(s_cast_b1, 1)
            ffn(0)
            dve.wait_ge(s_acc, 4)
            norm_stats(3)
            normalise(3)
            stream_lo(3)

            def bias_and_min(i, par, t):
                dve.wait_ge(s_scored, TB * i + t + 1)
                if t == 0:
                    dve.wait_ge(s_alibi, i + 1)
                u = t - 3
                need(dve, s_pt, NCH * i + FIRST[u] + len(CHUNKS[u]) if u >= 0
                     else NCH * (i - 1) + FIRST[TB + u] + len(CHUNKS[TB + u]))
                dve.memset(carrier[:, :], 0.0)
                k = P * (t + 1)
                dve.tensor_tensor_reduce(out=srow[:, P * ROW_AT[t]:P * ROW_AT[t] + k], in0=scores[:, 0:k], in1=alibi[:, par, T - k:T],
                                         scale=1.0, scalar=3e38, op0=ALU.add, op1=ALU.min,
                                         accum_out=neg_max[:, par, t:t + 1]).then_inc(s_ttr, 1)

            def pt_lo(i, t, chunks=(0, 1)):
                for c, (b0, nb) in enumerate(CHUNKS[t]):
                    if c not in chunks:
                        continue
                    ch = NCH * i + FIRST[t] + c
                    dve.wait_ge(s_pthi, ch + 1)
                    dve.tensor_tensor(pair_part(pT_lo, t, b0, nb), chunk_bank(t, c, nb),
                                      pair_part(pT_hi, t, b0, nb).bitcast(F32), ALU.subtract).then_inc(s_ptlo, 1)

            def x_lo(use, half, dst, hi, scale):
                dve.wait_ge(s_xhi, use + 1)
                dve.scalar_tensor_tensor(dst, ps[:, X_BANK[half], :], scale[:, :], hi.bitcast(F32), ALU.mult, ALU.subtract)\
                    .then_inc(s_xlo, 1)

            def half_of(tile, par, half):
                return tile[:, par, half * HT:(half + 1) * HT]

            def qk_sum(n, half):
                dve.wait_ge(s_sq, 2 * n + half + 1)
                dve.tensor_reduce(qk_ss[:, half, :], sq[:, :, :].rearrange("p b (a d) -> p (b a) d", a=2), AX_X,
                                  ALU.add).then_inc(s_qkss, 1)

            def y_lo(h, half):
                dve.wait_ge(s_yhi, 2 * h + half + 1)
                dve.wait_ge(s_ysq, 2 * h + half + 1)
                dst = (slice(None), half_columns(half))
                dve.scalar_tensor_tensor(yT_lo[dst], ps[:, Y_BANK[half], :], y_scale[:, :], yT_hi[dst].bitcast(F32),
                                         ALU.mult, ALU.subtract).then_inc(s_ylo, 1)

            def y_norm(h, par, part, halves, last_head):
                if part == 0:
                    sums = row_sum[:, par, :]
                    dve.scalar_tensor_tensor(y_e[:, :], sums, EPS, sums, ALU.mult, ALU.mult).then_inc(s_ye, 1)
                dve.wait_ge(s_yss, h + part + 1)
                dve.wait_ge(s_ye, h + 1)
                for half in halves:
                    last = dve.scalar_tensor_tensor(y_t[:, half_blocks(half)], y_sums(last_head, half), 1.0 / D,
                                                    y_e[:, half_blocks(half)], ALU.mult, ALU.add)
                last.then_inc(s_yt, 1)

            def add_projection(h, u, last_head):
                dve.wait_ge(s_pj, 4 * h + u + 1)
                if u == 0:
                    dve.wait_ge(s_yf, h + 1)
                if u == 2 and last_head:
                    dve.wait_ge(s_yf, h + 2)
                for k in range(2):
                    rows = x[:, 2 * u + k, :]
                    last = dve.scalar_tensor_tensor(rows, ps[:, M_BANK + u % 2, k * C:(k + 1) * C],
                                                    y_f[:, 2 * u + k:2 * u + k + 1], rows, ALU.mult, ALU.add)
                last.then_inc(s_pjadd, 1)

            def body(i, it, par):
                att, nxt, prev, after = parts(i)
                n = i + 1
                for t in range(TB):
                    if nxt and t == 7:
                        bias_and_min(n, 1 - par, 1)
                    if att and t < 7:
                        pt_lo(i, t)
                    if att and t == 7:
                        pt_lo(i, t, (0,))
                    if prev and t == 7:
                        add_projection(i - 1, 2, not att)
                    if att and t == 7:
                        y_lo(i, 0)
                        pt_lo(i, t, (1,))
                    if att and t < TB - 2:
                        bias_and_min(i, par, t + 2)
                    if att and t < 2:
                        lo, hi, pos, scale = ((kT_lo, kT_hi, KB, k_scale), (qT_lo, qT_hi, QB, q_scale))[t]
                        x_lo(xuse(i, pos), 1, half_of(lo, par, 1), half_of(hi, par, 1), scale)
                    if nxt and t in qk_steps(att):
                        lo, hi, pos, scale = ((kT_lo, kT_hi, KA, k_scale), (qT_lo, qT_hi, QA, q_scale))[
                            qk_steps(att).index(t)]
                        x_lo(xuse(i, pos), qk_bank(att, pos - KA), half_of(lo, 1 - par, 0), half_of(hi, 1 - par, 0),
                             scale)
                    if nxt and t == 2:
                        qk_sum(n, 0)
                    if prev and not att and t == 2:
                        y_norm(i - 1, 1 - par, 0, (0,), True)
                    if prev and t == 2:
                        y_lo(i - 1, 1)
                    if prev and att and t == 3:
                        y_norm(i - 1, 1 - par, 0, (0, 1), False)
                    if prev and not att and t == 3:
                        add_projection(i - 1, 0, True)
                        add_projection(i - 1, 1, True)
                        y_norm(i - 1, 1 - par, 1, (1,), True)
                        dve.wait_ge(s_pjadd, 4 * H - 2)
                        norm_stats(4)
                    if nxt and t == 6:
                        bias_and_min(n, 1 - par, 0)
                        qk_sum(n, 1)
                    if prev and t in ((4, 5, 7) if att else (7,)):
                        add_projection(i - 1, t - HB, not att)

            run_heads(dve, body)
            dve.wait_ge(s_pjadd, 4 * H)
            norm_stats(5)
            normalise(5)
            stream_lo(4)
            stream_lo(5)
            ffn(1)

        @block.tensor
        def _(pe):
            pe.wait_ge(s_const, 3)

            def transpose_stream(m):
                pe.wait_ge((s_xn0, s_xn)[m % 2], m // 2 + 1)
                for c in range(CC):
                    for b in range(HB):
                        last = pe.transpose(ps[:, 2 * (m % 2) + c, b * P:(b + 1) * P],
                                            xn[m % 2][:, b, c * P:(c + 1) * P], ident[:, :])
                    last.then_inc(s_xtr, 1)

            def ffn(f):
                pe.wait_ge(s_gw, 2)
                for half in range(2):
                    pe.wait_ge(s_xTlo, CC * (4 * f + half + 1))
                    for n, (c, part) in enumerate((c, part) for c in range(CC) for part in (xT_hi, xT_lo)):
                        last = pe.matmul(ps[:, G_BANK + half, :], gw2[:, c, :], part[:, c, half_columns(half)],
                                         start=n == 0, stop=n == 3)
                    last.then_inc(s_lgT, 1)
                for tb in range(TB):
                    if tb % HB == 0:
                        pe.wait_ge((s_lg0, s_lg1)[tb // HB], f + 1)
                    last = pe.transpose(ps[:, G_BANK, tb * 2 * E:(tb + 1) * 2 * E], lgT[:, tb * P:(tb + 1) * P],
                                        ident[0:2 * E, 0:2 * E])
                last.then_inc(s_logit, 1)

                def product(bank, weights, jt, half):
                    for n, (c, part) in enumerate((c, part) for c in range(CC) for part in (xT_hi, xT_lo)):
                        last = pe.matmul(ps[:, bank, :], weights[:, c, jt * P:(jt + 1) * P],
                                         part[:, c, half * HT:(half + 1) * HT], start=n == 0, stop=n == 3)
                    return last

                def combine_rows():
                    pe.wait_ge(s_rt_dve, RT_DVE * (f + 1))
                    for tb in range(TB):
                        last = pe.transpose(ps[:, G_BANK + tb // HB, (tb % HB) * P:(tb % HB + 1) * P],
                                            cw_rows[:, tb, :], ident[:, :])
                        if tb % HB == HB - 1:
                            last.then_inc(s_cwtr, 1)
                    pe.wait_ge(s_expert, 16)

                def up(g, half, jt):
                    if g == 0:
                        pe.wait_ge(s_cast_a, CC)
                    u = g - 2 * JT * f
                    if u >= 3:
                        pe.wait_ge(s_silu, 2 * JT * f + ab_before(u) + 1)
                    product(A_BANKS[ab_slot(u)], up_a, jt, half).then_inc(s_a, 1)
                    if g == 0:
                        pe.wait_ge(s_cast_b0, 1)
                        pe.wait_ge(s_cast_b1, 1)
                    if u >= 3:
                        pe.wait_ge(s_m, 2 * JT * f + ab_before(u) + 1)
                    product(B_BANKS[ab_slot(u)], up_b, jt, half).then_inc(s_b, 1)

                def spread(g, half, jt):
                    first = weighted_before(f, 0)
                    w = weighted_before(f, g - 2 * JT * f)
                    if w - first < 2:
                        pe.wait_ge(s_cwT, 2 * f + w - first + 1)
                    else:
                        pe.wait_ge(s_h, w - 1)
                    pe.matmul(ps[:, G_BANK + w % 2, :], expert_of[:, jt * P:(jt + 1) * P],
                              cwT[:, half * HT:(half + 1) * HT], start=True, stop=True).then_inc(s_g, 1)

                def back(g, half, jt):
                    if jt == TILES[0][0] and half == 0:
                        pe.wait_ge(s_cast_d, f + 1)
                    if jt == TILES[1][0] and half:
                        pe.wait_ge(s_acc, 4 * f + 2)
                    pe.wait_ge(s_hlo, g + 1)
                    for b in range(HB):
                        for part in (hT_hi, hT_lo):
                            last = pe.matmul(ps[:, ACC_BANK + b // 2, (b % 2) * C:(b % 2 + 1) * C],
                                             part[:, g % HRING, b * P:(b + 1) * P], down[:, jt, :],
                                             start=jt == TILES[half][0] and part is hT_hi and b % 2 == 0,
                                             stop=jt == TILES[half][-1] and part is hT_lo, skip_group_check=True)
                    last.then_inc(s_down, 1)

                units = [(2 * JT * f + JT * half + n, half, jt) for half in range(2) for n, jt in enumerate(TILES[half])]
                for step in range(2 * JT + LAG):
                    d = step - LAG
                    if step < 2 * JT:
                        up(*units[step])
                    if d == 0:
                        combine_rows()
                    if d >= 0 and weighted(d):
                        spread(*units[d])
                    if d >= 2:
                        back(*units[d - 2])
                    if f == 0 and step == 2 * JT + 2:
                        transpose_stream(2)
                back(*units[-2])
                back(*units[-1])

            transpose_stream(0)
            transpose_stream(1)
            ffn(0)

            def score(i, par, t):
                if t == 0:
                    pe.wait_ge(s_xlo, xuse(i - 1, QA) + 1)
                if t == HB:
                    pe.wait_ge(s_xlo, xuse(i, QB) + 1)
                need(pe, s_ttr, TB * i + t)
                q = slice(t * P, (t + 1) * P)
                for c0 in range(0, t + 1, 4):
                    k = slice(c0 * P, min(t + 1, c0 + 4) * P)
                    for n, (a, b) in enumerate(((qT_hi, kT_hi), (qT_hi, kT_lo), (qT_lo, kT_hi))):
                        last = pe.matmul(scores[:, k], a[:, par, q], b[:, par, k], start=n == 0, stop=n == 2)
                last.then_inc(s_scored, 1)

            def project_qkv(n, tb):
                if tb == 0:
                    pe.wait_ge(s_wlo, n + 1)
                if isinstance(n, int) and n == 0 and tb % HB == 0:
                    if tb:
                        transpose_stream(3)
                    pe.wait_ge(s_xTlo, CC * (3 + tb // HB))
                if tb < 2:
                    need(pe, s_pjadd, 4 * (n - 2) - 1 + tb)
                else:
                    need(pe, s_row, TB * n + tb - 1)
                last_of = 3 * CC - 1
                m = 0
                for c in range(CC):
                    for a, b in ((xT_hi, w_hi), (xT_hi, w_lo), (xT_lo, w_hi)):
                        last = pe.matmul(ps[:, M_BANK + tb % 2, 0:3 * D], a[:, c, tb * P:(tb + 1) * P], b[:, c, :],
                                         start=m == 0, stop=m == last_of)
                        m += 1
                last.then_inc(s_qkv, 1)

            def transpose_p(i, t):
                pe.wait_ge(s_exp, TB * i + t + 1)
                for c, (b0, nb) in enumerate(CHUNKS[t]):
                    need(pe, s_ptlo, NCH * i + FIRST[t] + c - 1)
                    for b in range(nb):
                        last = pe.transpose(ps[:, PT_BANK + (FIRST[t] + c) % 2, b * P:(b + 1) * P],
                                            srow[:, (ROW_AT[t] + b0 + b) * P:(ROW_AT[t] + b0 + b + 1) * P],
                                            ident[:, :])
                    last.then_inc(s_pt, 1)

            def values(i, par, u, part, has_next=True):
                if part == 0:
                    if u == 0:
                        pe.wait_ge(s_vlo, i + 1)
                        pe.wait_ge(s_xlo, xuse(i, QB) + 1)
                    if u == 2:
                        pe.wait_ge(s_xlo, xuse(i, QA) + 1 if has_next else xuse(i, QB) + 1)
                        need(pe, s_yt, i)
                    t = 2 * u + 1
                    pe.wait_ge(s_ptlo, NCH * i + FIRST[t] + len(CHUNKS[t]))
                blocks = 2 * u + 2
                for s in range(part * (u + 1), (part + 1) * (u + 1)):
                    first = P if s == blocks - 1 else 0
                    out_ = ps[:, Y_BANK[u // 2], (u % 2) * 2 * P + first:(u % 2 + 1) * 2 * P]
                    for m, (a, b) in enumerate(((v_hi, pT_hi), (v_hi, pT_lo), (v_lo, pT_hi))):
                        last = pe.matmul(out_, a[:, par, s, :], b[:, PAIR_AT[u] + s, first:],
                                         start=s == 0 and m == 0, stop=s == blocks - 1 and m == 2,
                                         skip_group_check=True)
                if u % 2 and part:
                    last.then_inc(s_pv, 1)

            def sum_squares(h, half, last_head):
                if last_head:
                    pe.wait_ge(s_ysq, 2 * h + half + 1)
                else:
                    pe.wait_ge(s_ylo, 2 * (h + 1))
                for b in range(HB):
                    tb = half * HB + b
                    last = pe.matmul(y_sums(last_head, half)[:, b:b + 1], ysq[:, tb * P:(tb + 1) * P], ones[:, :],
                                     start=True, stop=True)
                if half or last_head:
                    last.then_inc(s_yss, 1)

            def transpose_half(use, half, ready, count, blocks):
                pe.wait_ge(ready, count)
                need(pe, s_xlo, use)
                for b, block_ in enumerate(blocks):
                    last = pe.transpose(ps[:, X_BANK[half], b * P:(b + 1) * P], block_, ident[:, :])
                last.then_inc(s_xt, 1)

            def qk_blocks(half, which):
                return [qkv[:, half * HB + b, which * D:(which + 1) * D] for b in range(HB)]

            def project_y(h, q, rows):
                if q == 0:
                    pe.wait_ge(s_wplo, h + 1)
                if q % 2 == 0:
                    pe.wait_ge(s_ylo, 2 * h + q // 2 + 1)
                if q < 2 and rows is not None:
                    need(pe, s_row, rows + q)
                else:
                    need(pe, s_pjadd, 4 * h + q - 1)
                for k in range(2):
                    b = 2 * q + k
                    for m, (a, w) in enumerate(((yT_hi, wp_hi), (yT_hi, wp_lo), (yT_lo, wp_hi))):
                        last = pe.matmul(ps[:, M_BANK + q % 2, k * C:(k + 1) * C], a[:, b * P:(b + 1) * P], w[:, :],
                                         start=m == 0, stop=m == 2)
                last.then_inc(s_pj, 1)

            def body(i, it, par):
                att, nxt, prev, after = parts(i)
                n = i + 1
                for t in range(TB):
                    if att:
                        transpose_p(i, t)
                    if att and t < TB - 2:
                        score(i, par, t + 2)
                    if nxt and t < HB:
                        project_qkv(n, 2 * t)
                    if att and t < 2:
                        if t == 0:
                            need(pe, s_ylo, 2 * (i - 1) + 1)
                        transpose_half(xuse(i, (KB, QB)[t]), 1, s_qkn, 2 * i + 2, qk_blocks(1, 1 - t))
                    if nxt and t in qk_steps(att):
                        if prev and t == 4:
                            pe.wait_ge(s_yt, i)
                        which = qk_steps(att).index(t)
                        transpose_half(xuse(i, (KA, QA)[which]) if att else 0, qk_bank(att, which), s_qkn, 2 * n + 1,
                                       qk_blocks(0, 1 - which))
                    if nxt and t == 7:
                        score(n, 1 - par, 1)
                    if prev and not att and t == 2:
                        sum_squares(i - 1, 0, True)
                    if prev:
                        for q in projections_at(att, t):
                            project_y(i - 1, q, TB * n + 7 if nxt else TB * H - 1 if att else None)
                    if nxt and t == 6:
                        score(n, 1 - par, 0)
                    if prev and t < 2:
                        values(i - 1, 1 - par, 3, t)
                    if att and t > 1:
                        values(i, par, (t - 2) // 2, t % 2, nxt)
                    if nxt and t < HB:
                        project_qkv(n, 2 * t + 1)
                    if prev and t == 3:
                        for half in ((0, 1) if att else (1,)):
                            sum_squares(i - 1, half, not att)

            run_heads(pe, body)
            transpose_stream(4)
            transpose_stream(5)
            ffn(1)


def kernel(**inputs):
    import concourse.bacc as bacc
    from concourse.bass_utils import run_bass_kernel_spmd

    g = {k.removeprefix("L0_"): np.asarray(v) for k, v in inputs.items()}
    x = g["attn_x"]
    _, T, C = x.shape
    H, D = 16, P
    E = g["ffn_gate_w"].shape[0]

    def heads(w):
        return w.reshape(C // P, P, H, D).transpose(2, 1, 0, 3)

    def columns(w, shared):
        return np.concatenate([w.reshape(-1, C), shared], axis=0).T

    arrays = {
        "x_in": x.reshape(T, C),
        "w_qkv": np.concatenate([heads(g["attn_Wq"]), heads(g["attn_Wk"]), heads(g["attn_Wv"])], axis=3),
        "w_proj": g["attn_Wproj"].reshape(H, D, C),
        "q_w": g["attn_q_rms_w"].reshape(D, 1),
        "k_w": g["attn_k_rms_w"].reshape(D, 1),
        "y_w": g["attn_subln_w"].reshape(D, 1),
        "gate_w": g["ffn_gate_w"].T,
        "gate_b": np.tile(g["ffn_gate_b"], (P, T // P)),
        "w_up_a": columns(g["ffn_w1"], g["ffn_sw1"]),
        "w_up_b": columns(g["ffn_w3"], g["ffn_sw3"]),
        "w_down": np.concatenate([g["ffn_w2"].transpose(0, 2, 1).reshape(-1, C), g["ffn_sw2"].T], axis=0),
    }
    arrays = {k: np.ascontiguousarray(v) for k, v in arrays.items()}
    nc = bacc.Bacc("TRN2", target_bir_lowering=False, num_devices=1)
    aps = [nc.dram_tensor(k, v.shape, mybir.dt.from_np(v.dtype), kind="ExternalInput").ap() for k, v in arrays.items()]
    out = nc.dram_tensor("out", (T, C), F32, kind="ExternalOutput").ap()
    macaron_kernel(nc, *aps, out)
    result = run_bass_kernel_spmd(nc, [arrays], core_ids=[0])
    return result.results[0]["out"].reshape(x.shape)
```
